# Optimizing a Trainium2 kernel written in Bass

```python
import numpy as np
import jax
import jax.numpy as jnp

def _softmax(x, axis=-1):
    return jax.nn.softmax(x, axis=axis)
def _gelu(x):
    return jax.nn.gelu(x, approximate=True)
def _silu(x):
    return jax.nn.silu(x)
def _sigmoid(x):
    return jax.nn.sigmoid(x)
def _layernorm(x, axis=-1, eps=1e-5):
    m = jnp.mean(x, axis=axis, keepdims=True)
    v = jnp.var(x, axis=axis, keepdims=True)
    return (x - m) / jnp.sqrt(v + eps)
def _scatter_add(tgt, idx, src, axis=0):
    return tgt.at[idx].add(src)
def _segment_sum(src, seg, n):
    return jax.ops.segment_sum(src, seg, n)

kernel_name = 'mk_adj_resnorm_d4_adj_64_c667c9'

def setup_inputs(seed: int = 0):
    np.random.seed(seed)
    _w = jnp.asarray
    def _rec_inputs():
        import jax
        import jax.numpy as jnp
        _gk = jax.random.key(seed)
        x = -0.0002928 + 1 * jax.random.normal(jax.random.fold_in(_gk, 1), (8, 2048, 64), jnp.float32)
        _a = jax.random.bernoulli(jax.random.fold_in(_gk, 2), 0.00390625, (2048, 2048))
        _a = jnp.logical_or(_a, jnp.swapaxes(_a, -1, -2))
        _a = jnp.logical_or(_a, jnp.eye(2048, dtype=bool))
        _af = _a.astype(jnp.float32)
        _af = _af / jnp.maximum(_af.sum(-1, keepdims=True), 1.0)
        adj = _af
        return x, adj
    x, adj = _rec_inputs()
    def _L0_gnn_setup():
        import jax, jax.numpy as jnp
        import numpy as np
        key = jax.random.key(seed)
        ks = jax.random.split(key, 5)
        B, N, IN, OUT, K, D = (32, 2048, 64, 64, 3, 16)
        x = jax.random.normal(ks[0], (B, N, IN), dtype=jnp.float32)
        A = jax.random.uniform(ks[1], (N, N), dtype=jnp.float32)
        A = A / jnp.sum(A, axis=-1, keepdims=True)
        embedding = jax.random.normal(ks[2], (N, D), dtype=jnp.float32) * 0.3
        weight = jax.random.normal(ks[3], (D, K, IN, OUT), dtype=jnp.float32) * 0.1
        bias = jax.random.normal(ks[4], (D, OUT), dtype=jnp.float32) * 0.1
        return {'x': x, 'A': A, 'embedding': embedding, 'weight': weight, 'bias': bias}
    _L0_gnn_all = _L0_gnn_setup()
    _L0_gnn_in = {k: v for k, v in _L0_gnn_all.items() if k in ('embedding', 'weight', 'bias', )}
    del _L0_gnn_all

    def _L1_gnn_setup():
        import jax, jax.numpy as jnp
        import numpy as np
        B, N, C = (4, 4096, 64)
        ALPHA = 0.2
        THRESHOLD = 0.5
        NEG_INF = -9000000000000000.0
        key = jax.random.key(seed)
        k1, k2, k3 = jax.random.split(key, 3)
        inp = jax.random.normal(k1, (B, N, C), dtype=jnp.float32)
        adj = jax.random.uniform(k2, (N, N), dtype=jnp.float32)
        bound = 1.414 * float(np.sqrt(6.0 / (2 * C + 1)))
        a = jax.random.uniform(k3, (2 * C, 1), dtype=jnp.float32, minval=-bound, maxval=bound)
        return {'input': inp, 'adj': adj, 'a': a}
    _L1_gnn_all = _L1_gnn_setup()
    _L1_gnn_in = {k: v for k, v in _L1_gnn_all.items() if k in ('a', )}
    del _L1_gnn_all

    def _L2_gnn_setup():
        import jax, jax.numpy as jnp
        import numpy as np
        NUM_NODE = 4096
        N_IN = 64
        N_HID = 64
        BATCH = 8
        key = jax.random.key(seed)
        k1, k2, k3, k4 = jax.random.split(key, 4)
        x = jax.random.normal(k1, (BATCH, NUM_NODE, N_IN), dtype=jnp.float32)
        adj = jax.random.uniform(k2, (NUM_NODE, NUM_NODE), dtype=jnp.float32)
        W = jax.random.normal(k3, (N_HID, N_IN), dtype=jnp.float32) * (1.0 / np.sqrt(N_IN))
        b = jax.random.normal(k4, (N_HID,), dtype=jnp.float32) * 0.01
        return {'x': x, 'adj': adj, 'W': W, 'b': b}
    _L2_gnn_all = _L2_gnn_setup()
    _L2_gnn_in = {k: v for k, v in _L2_gnn_all.items() if k in ('W', 'b', )}
    del _L2_gnn_all

    def _L3_gnn_setup():
        import jax, jax.numpy as jnp
        import numpy as np
        MAX_STEPS = 3
        key = jax.random.key(seed)
        ks = jax.random.split(key, 7)
        B, N, D = (1, 8192, 64)
        return {'causal_vars': jax.random.normal(ks[0], (B, N, D), dtype=jnp.float32), 'adj_matrix': jax.random.uniform(ks[1], (N, N), dtype=jnp.float32), 'intervention_value': jax.random.normal(ks[2], (B, D), dtype=jnp.float32), 'W1': jax.random.normal(ks[3], (D, 2 * D), dtype=jnp.float32) * (1.0 / np.sqrt(2 * D)), 'b1': jax.random.normal(ks[4], (D,), dtype=jnp.float32) * 0.01, 'W2': jax.random.normal(ks[5], (D, D), dtype=jnp.float32) * (1.0 / np.sqrt(D)), 'b2': jax.random.normal(ks[6], (D,), dtype=jnp.float32) * 0.01, 'intervention_idx': 0}
    _L3_gnn_all = _L3_gnn_setup()
    _L3_gnn_in = {k: v for k, v in _L3_gnn_all.items() if k in ('intervention_value', 'W1', 'b1', 'W2', 'b2', )}
    del _L3_gnn_all

    return {
        "x": x,
        "adj": adj,
        "L0_gnn_embedding": _L0_gnn_in["embedding"],
        "L0_gnn_weight": _L0_gnn_in["weight"],
        "L0_gnn_bias": _L0_gnn_in["bias"],
        "L1_gnn_a": _L1_gnn_in["a"],
        "L2_gnn_W": _L2_gnn_in["W"],
        "L2_gnn_b": _L2_gnn_in["b"],
        "L3_gnn_intervention_value": _L3_gnn_in["intervention_value"],
        "L3_gnn_W1": _L3_gnn_in["W1"],
        "L3_gnn_b1": _L3_gnn_in["b1"],
        "L3_gnn_W2": _L3_gnn_in["W2"],
        "L3_gnn_b2": _L3_gnn_in["b2"],
    }

def reference(x, adj, L0_gnn_embedding, L0_gnn_weight, L0_gnn_bias, L1_gnn_a, L2_gnn_W, L2_gnn_b, L3_gnn_intervention_value, L3_gnn_W1, L3_gnn_b1, L3_gnn_W2, L3_gnn_b2):
    import jax
    import jax.numpy as jnp
    def _L0_gnn_ref(x, A, embedding, weight, bias):
        import jax, jax.numpy as jnp
        import numpy as np
        K = weight.shape[1]
        N = A.shape[-2]
        w = jnp.einsum('nd,dkio->nkio', embedding, weight)
        b = jnp.einsum('nd,do->no', embedding, bias)
        As = [jnp.eye(N, dtype=x.dtype)]
        if K > 1:
            As.append(A)
        for _ in range(2, K):
            As.append(2.0 * (A @ As[-1]) - As[-2])
        A_stack = jnp.stack(As, 0)
        x_g = jnp.einsum('knm,bmc->bnkc', A_stack, x)
        out = jnp.einsum('bnki,nkio->bno', x_g, w)
        return out + b

    def _L1_gnn_ref(input, adj, a):
        import jax, jax.numpy as jnp
        import numpy as np
        B, N, C = (4, 4096, 64)
        ALPHA = 0.2
        THRESHOLD = 0.5
        NEG_INF = -9000000000000000.0
        h = input
        a1 = a[:C, 0]
        a2 = a[C:, 0]
        s1 = h @ a1
        s2 = h @ a2
        e = s1[:, :, None] + s2[:, None, :]
        e = jnp.where(e > 0, e, ALPHA * e)
        mask = adj[None, :, :] > THRESHOLD
        att = jnp.where(mask, e, NEG_INF)
        att = jax.nn.softmax(att, axis=2)
        h_prime = jnp.einsum('bij,bjc->bic', att, h)
        return jax.nn.elu(h_prime)

    def _L2_gnn_ref(x, adj, W, b):
        import jax, jax.numpy as jnp
        import numpy as np
        NUM_NODE = 4096
        N_IN = 64
        N_HID = 64
        BATCH = 8
        N = adj.shape[0]
        adj_i = adj + jnp.eye(N, dtype=adj.dtype)
        deg = jnp.sum(adj_i, axis=1, keepdims=True)
        emb = jnp.einsum('bnf,hf->bnh', x, W) + b
        agg = jnp.einsum('ij,bjh->bih', adj_i, emb) / deg
        return agg

    def _L3_gnn_ref(causal_vars, adj_matrix, intervention_value, W1, b1, W2, b2, intervention_idx):
        import jax, jax.numpy as jnp
        import numpy as np
        MAX_STEPS = 3
        v = causal_vars.at[:, intervention_idx].set(intervention_value)
        for _ in range(MAX_STEPS):
            effects = jnp.einsum('nm,bmd->bnd', adj_matrix, v)
            h = jnp.concatenate([v, effects], axis=-1)
            h = jax.nn.relu(jnp.einsum('bnk,dk->bnd', h, W1) + b1)
            v = jnp.einsum('bnk,dk->bnd', h, W2) + b2
        return v

    x = _layernorm(x + _L0_gnn_ref(x, adj, L0_gnn_embedding, L0_gnn_weight, L0_gnn_bias), axis=-1)
    x = _layernorm(x + _L1_gnn_ref(x, adj, L1_gnn_a), axis=-1)
    x = _layernorm(x + _L2_gnn_ref(x, adj, L2_gnn_W, L2_gnn_b), axis=-1)
    x = _layernorm(x + _L3_gnn_ref(x, adj, L3_gnn_intervention_value, L3_gnn_W1, L3_gnn_b1, L3_gnn_W2, L3_gnn_b2, 0), axis=-1)
    return x


_drawn_inputs = setup_inputs


def setup_inputs(seed=0):
    import zlib

    import numpy as np

    out = dict(_drawn_inputs(seed))
    spreads = {}
    factors = {'L2_gnn_b': 5.182,
     'L3_gnn_intervention_value': 36.759,
     'L3_gnn_b1': 5.294,
     'L3_gnn_b2': 3.497}
    for name, (base, spread) in spreads.items():
        noise = np.random.default_rng([zlib.crc32(name.encode()), seed]).standard_normal(out[name].shape)
        drawn = base * np.exp(spread * noise) if base else spread * noise
        out[name] = jnp.asarray(drawn.astype(out[name].dtype))
    for name, factor in factors.items():
        out[name] = (out[name] * factor).astype(out[name].dtype)
    return out
```

```python
import numpy as np
import concourse.bass as bass
from concourse import mybir
from contextlib import ExitStack

F32 = mybir.dt.float32
F16 = mybir.dt.float16
I32 = mybir.dt.int32
ALU = mybir.AluOpType
ACT = mybir.ActivationFunctionType
AX = mybir.AxisListType

NT = 16
B, C, D = 8, 64, 16
BC = B * C
N = 2048
PE, AC, DV, PO, SP = "tensor", "scalar", "vector", "gpsimd", "sync"
ENGINES = (PE, AC, DV, PO, SP)


class Tok:

    def __init__(self, section, sem=None, val=0):
        self.section, self.sem, self.val, self.used = section, sem, val, False


def tokens(waits):
    for w in waits:
        if isinstance(w, (list, tuple)):
            yield from tokens(w)
        elif w is not None:
            yield w


class Queues:

    def __init__(self, sems):
        self.q = {e: [] for e in ENGINES}
        self.sems = sems
        self.section = None
        self.dma = {}

    def op(self, eng, fn, *waits):
        tok = Tok(self.section)
        flat = list(tokens(waits))
        for w in flat:
            assert w.section is None or w.section == self.section, "a wait on what may not run"
            w.used = True
        self.q[eng].append((self.section, fn, flat, tok))
        return tok

    def load(self, eng, out, in_, sem, *waits):
        tok = Tok(self.section, sem, self.dma.get(id(sem), 0) + 16)
        self.dma[id(sem)] = tok.val
        self.op(eng, lambda e: (e.dma_start(out, in_).then_inc(sem, 16), None)[1], *waits)
        return tok

    def number(self):
        for eng in ENGINES:
            count = {}
            for section, _, _, tok in self.q[eng]:
                if tok.used and tok.sem is None:
                    count[section] = count.get(section, 0) + 1
                    tok.sem, tok.val = self.sems[eng, section], count[section]

    def replay(self, eng, e, flags):
        seen = {}
        items, k = self.q[eng], 0

        def emit(item, seen):
            _, fn, waits, tok = item
            need = {}
            for w in waits:
                if seen.get(id(w.sem), 0) < w.val:
                    need[id(w.sem)] = (w.sem, max(w.val, need.get(id(w.sem), (0, 0))[1]))
            for key, (sem, val) in need.items():
                e.wait_ge(sem, val)
                seen[key] = val
            ins = fn(e)
            if tok.used:
                ins.then_inc(tok.sem, 1)

        while k < len(items):
            section = items[k][0]
            end = k
            while end < len(items) and items[end][0] == section:
                end += 1
            if section is None:
                for item in items[k:end]:
                    emit(item, seen)
            else:
                with e.If(flags[eng, section]()):
                    inner = dict(seen)
                    for item in items[k:end]:
                        emit(item, inner)
            k = end


def gnn_kernel(nc, x_in, at_in, a_in, embt_in, emb_in, w0_in, w0b_in, wl_in, w1t_in, w2t_in,
               w1_in, w2_in, b1_in, rows_in, out):
    ctx = ExitStack()
    with ctx:
        def sb(name, shape, dt):
            return ctx.enter_context(nc.sbuf_tensor(name, shape, dt))

        def sem(name):
            return ctx.enter_context(nc.semaphore(name))

        Bm = sb("Bm", [128, NT, N], F16)
        S0 = sb("S0", [128, NT, 1024], F16)
        S1 = sb("S1", [128, NT, 1024], F16)
        X = sb("X", [128, NT, BC], F32)
        R = sb("R", [128, 3, N], F32)
        W01 = sb("W01", [128, 2, 1024], F16)
        W2 = sb("W2", [128, 2, 1024], F16)
        T3 = sb("T3", [128, 3072], F32)
        M2 = sb("M2", [128, 2048], F32)
        bdh = sb("bdh", [128, 4, 128], F16)
        bdl = sb("bdl", [128, 4, 128], F16)
        i16 = sb("i16", [128, 128], F16)
        i32 = sb("i32", [128, 128], F32)
        ones = sb("ones", [128, 128], F32)
        emb = sb("emb", [128, NT, D], F32)
        rows = sb("rows", [128, 5, C], F32)
        b1c = sb("b1c", [128, 1], F32)
        b1s = sb("b1s", [128, 3], F32)
        b2s = sb("b2s", [128, 4, C], F32)
        nrm = sb("nrm", [128, 3, C], F32)
        st = sb("st", [128, 12], F32)
        sr = sb("sr", [128, 12], F32)
        fl = sb("fl", [128, 5], F32)
        fr = sb("fr", [128, 5], F32)
        fi = sb("fi", [128, 2], I32)
        cs = sb("cs", [128, 64], F32)
        ra = sb("ra", [128, 8, NT], F32)
        xm = sb("xm", [128, NT], F32)
        sm = sb("sm", [128, 2, 32], F32)
        PS = ctx.enter_context(nc.psum_tensor("PS", [128, 4096], F32))

        blo = nc.dram_tensor("blo", [NT, 128, NT, 128], F16, kind="Internal").ap()

        vmx = sb("vmx", [128, NT], F32)
        vm = [None] * NT
        rmax, rmin, nr, sg1, sg0, deg, r2, cw = (ra[:, k, :] for k in range(8))

        def bank(b):
            return PS[:, b * 512:(b + 1) * 512]

        def bank16(b):
            return bank(b).bitcast(F16)

        def col(k):
            return cs[:, k:k + 1]

        def grid(ap, n=C):
            return ap.rearrange("p (b c) -> p b c", c=n)

        def spread(ap8):
            return ap8.unsqueeze(2).broadcast_to([128, B, C])

        def each_b(ap64):
            return ap64.unsqueeze(1).broadcast_to([128, B, C])

        sems = {(e, s): sem(f"s_{e}_{s}") for e in ENGINES for s in (None, "G", "H")}
        Q = Queues(sems)
        s_ring = [sem(f"s_ring{k}") for k in range(3)]
        s_x = [sem(f"s_x{k}") for k in range(4)]
        s_small = [sem(f"s_small{k}") for k in range(17)]
        s_gr = [sem(f"s_gr{k}") for k in range(3)]
        s_gw = sem("s_gw")
        s_gb = [sem(f"s_gb{k}") for k in range(2)]
        s_h = sem("s_h")
        s_out = [sem(f"s_out{k}") for k in range(2)]

        def pe(fn, *w): return Q.op(PE, fn, *w)
        def act(fn, *w): return Q.op(AC, fn, *w)
        def dve(fn, *w): return Q.op(DV, fn, *w)
        def pool(fn, *w): return Q.op(PO, fn, *w)

        def mm(o, l, r, start, stop, *w):
            return pe(lambda e: e.matmul(o, l, r, start=start, stop=stop), *w)

        def transpose(o, i, ident, *w):
            return pe(lambda e: e.transpose(o, i, ident), *w)

        def ts(o, i, s1, s2, o1, o2, *w, on=DV):
            return Q.op(on, lambda e: e.tensor_scalar(o, i, s1, s2, o1, o2) if o2 is not None
                        else e.tensor_scalar(o, i, s1, None, o1), *w)

        def tt(o, a, b, f, *w, on=DV):
            return Q.op(on, lambda e: e.tensor_tensor(o, a, b, f), *w)

        def stt(o, a, s, b, f, g, *w):
            return dve(lambda e: e.scalar_tensor_tensor(out=o, in0=a, scalar=s, in1=b, op0=f, op1=g), *w)

        def red(o, i, f, *w, absolute=False):
            return dve(lambda e: e.tensor_reduce(o, i, op=f, axis=AX.X, apply_absolute_value=absolute), *w)

        def fn(o, i, func, *w, **kw):
            return act(lambda e: e.activation(o, i, func, **kw), *w)

        def copy(on, o, i, *w):
            if on == AC:
                return fn(o, i, ACT.Copy, *w)
            return Q.op(on, lambda e: e.tensor_copy(o, i), *w)

        bfree = {b: [] for b in range(8)}
        unread = {b: False for b in range(8)}

        z0 = pool(lambda e: e.memset(i32[:, :], 0.0))
        z1 = pool(lambda e: e.memset(ones[:, :], 1.0))
        k_i32 = pool(lambda e: e.affine_select(out=i32[:, :], in_=i32[:, :], compare_op=ALU.not_equal, fill=1.0,
                                               base=0, pattern=[[-1, 128]], channel_multiplier=1), z0)
        k_i16 = pool(lambda e: e.tensor_copy(i16[:, :], i32[:, :]), k_i32)
        k_one = z1
        k_st = pool(lambda e: e.memset(st[:, :], 0.0))
        bds = M2[:, 1536:2048].rearrange("p (k m) -> p k m", k=4)
        z_bd = pool(lambda e: e.memset(bds, 0.0))

        Wa, Wb = T3[:, 0:1024], T3[:, 1024:2048]
        NB = T3[:, 2048:3072].rearrange("p (t c) -> p t c", c=C)
        embt = T3[0:D, 0:1536]
        embt2 = M2[0:D, 0:512]
        xr = x_in.rearrange("(t p) c -> t p c", p=128)
        atr = at_in.rearrange("(t p) i -> t p i", p=128)
        ar = a_in.rearrange("(t p) j -> t p j", p=128)

        x_ready, at_ready, b_done = [], [], []
        small = iter(s_small)

        def load_small(o, i, *w):
            return Q.load(AC, o, i, next(small), *w)

        for jt in range(NT):
            x_ready.append(Q.load(AC, X[:, jt, :], xr[jt], s_x[jt % 4],
                                  x_ready[jt - 4] if jt >= 4 else None))
            if jt == 0:
                l_emb = load_small(emb[:, :, :], emb_in.rearrange("(t p) d -> p t d", p=128))
                l_et = load_small(embt, embt_in[:, 0:1536])
                l_et2 = load_small(embt2, embt_in[:, 1536:2048])
                l_rows = load_small(rows[:, :, :], rows_in.rearrange("p (k c) -> p k c", c=C))
                l_bias = load_small(nrm[0:D, 2, :], w0b_in)
                l_b1 = load_small(b1c[:, :], b1_in)
                l_w1n = load_small(nrm[0:64, 0:2, :], w1_in.rearrange("p (k c) -> p k c", c=C))
        l_bd = []
        for k, src in enumerate((w1t_in[0:64, :], w1t_in[64:128, :], w2t_in, wl_in)):
            for h in range(2):
                l_bd.append(load_small(bds[64 * h:64 * h + 64, k, 64 * h:64 * h + 64], src, z_bd))

        for t in range(NT):
            src = embt[:, t * 128:(t + 1) * 128] if t < 12 else embt2[:, (t - 12) * 128:(t - 11) * 128]
            k_nb = mm(PS[:, 3072 + t * C:3072 + (t + 1) * C], src, nrm[0:D, 2, :], True, True,
                      l_et, l_et2, l_bias)
        c_nb = copy(DV, T3[:, 2048:3072], PS[:, 3072:4096], k_nb)
        l_wa = load_small(Wa, w0_in[0:128, :], k_nb)
        s_wb = [sem("s_wb0"), sem("s_wb1")]
        l_wb = [Q.load(AC, T3[64 * h:64 * h + 64, 1024:2048], w0_in[128:192, :], s_wb[h], k_nb) for h in range(2)]
        l_w2n = Q.load(AC, nrm[0:64, 2, :], w2_in, s_wb[0], k_nb, l_wb[0])

        SX = 64.0
        p0 = [None] * NT

        def xpart(S, jt):
            return S[:, jt, :].rearrange("p (b k c) -> p b k c", k=2, c=C)[:, :, 0, :]

        def tpart(S, jt):
            return S[:, jt, :].rearrange("p (b k c) -> p b k c", k=2, c=C)[:, :, 1, :]

        def split(jt, scale, *w):
            a = fn(xpart(S0, jt), grid(X[:, jt, :]), ACT.Copy, *w, scale=scale)
            return stt(xpart(S1, jt), grid(X[:, jt, :]), scale, xpart(S0, jt), ALU.mult, ALU.subtract, a, *w)

        bfree[6].append(c_nb)
        bfree[7].append(c_nb)

        ring_tok = [None] * 3
        nring = 0

        def ring(src):
            nonlocal nring
            k = nring % 3
            nring += 1
            return k, Q.load(SP, R[:, k, :], src, s_ring[k], ring_tok[k])

        last = {}

        def pair(b, it, jt, rh, rl, *w):
            mm(bank(b), Bm[:, jt, it * 128:(it + 1) * 128], rh(jt), jt == 0, False, *w)
            return mm(bank(b), Bm[:, jt, it * 128:(it + 1) * 128], rl(jt), False, jt == NT - 1)

        gload = {"n": 0, "tok": [None, None], "saved": None}

        def low_pass(tiles, banks, rh, *w):
            keep = Q.section
            Q.section = "G"
            for it, b in zip(tiles, banks):
                k = gload["n"] % 2
                gload["n"] += 1
                dst = R[:, 2, k * 1024:(k + 1) * 1024].bitcast(F16).rearrange("p (t i) -> p t i", i=128)
                ld = Q.load(SP, dst, blo[it], s_gb[k], gload["tok"][k], gload["saved"])
                for jt in range(NT):
                    m = mm(bank(b), dst[:, jt, :], rh(jt), False, False, ld, *w)
                gload["tok"][k] = m
            Q.section = keep

        class Tasks:

            def __init__(self, width=2):
                self.wait, self.active, self.turn, self.width = [], [], 0, width

            def add(self, gen):
                self.wait.append(gen)

            def slot(self):
                while len(self.active) < self.width and self.wait:
                    self.active.append(self.wait.pop(0))
                if not self.active:
                    return False
                self.turn += 1
                g = self.active[self.turn % len(self.active)]
                if next(g, "end") == "end":
                    self.active.remove(g)
                return True

            def until(self, cond):
                while not cond():
                    assert self.slot()

        def product(first, singles, banks, rh, rl, ready, evac, tasks, mid=None, every=4, w=()):
            fb = banks[:len(first)]
            n = 0
            for jt in range(NT):
                if jt == NT - 1:
                    tasks.until(lambda: ready(jt) is not None)
                    low_pass(first, fb, rh, [ready(j) for j in range(NT)], *w)
                for it, b in zip(first, fb):
                    if jt == 0:
                        tasks.until(lambda: not unread[b])
                    if ready(jt) is None:
                        tasks.until(lambda: ready(jt) is not None)
                    t = pair(b, it, jt, rh, rl, ready(jt), bfree[b] if jt == 0 else None, *w)
                    last[it] = t
                    n += 2
                    if n % every == 0:
                        tasks.slot()
            if mid is not None:
                mid()
            for it, b in zip(first, fb):
                evac(it, b, last[it])
            for k, it in enumerate(singles):
                b = banks[k % len(banks)]
                tasks.until(lambda: not unread[b])
                for jt in range(NT):
                    if jt == NT - 1:
                        low_pass([it], [b], rh, *w)
                    t = pair(b, it, jt, rh, rl, bfree[b] if jt == 0 else None, *w)
                    n += 2
                    if n % every == 0:
                        tasks.slot()
                evac(it, b, t)

        xdone = [None] * NT
        for jt in range(NT):
            k, tok = ring(atr[jt])
            b01 = ts(Bm[:, jt, :], R[:, k, :], 0.0, None, ALU.not_equal, None, tok)
            ring_tok[k] = b01
            xt = split(jt, SX, x_ready[jt])
            mx = red(xm[:, jt:jt + 1], X[:, jt, :], ALU.max, absolute=True)
            p0[jt] = [b01, xt]

        def rx(S):
            return lambda jt: xpart(S, jt)

        st_r = [None] * NT
        junk = M2[:, 0:1024].bitcast(F16)
        jtok = k_nb

        def row_stats(it):
            nonlocal jtok
            k, tok = ring(ar[it])
            a = red(rmax[:, it:it + 1], R[:, k, :], ALU.max, tok)
            n1 = ts(nr[:, it:it + 1], rmax[:, it:it + 1], -1.0, None, ALU.mult, None, a)
            b = red(rmin[:, it:it + 1], R[:, k, :], ALU.min)
            c = fn(junk, R[:, k, :], ACT.Sign, tok, n1, jtok, bias=nr[:, it:it + 1],
                   accum_out=sg1[:, it:it + 1])
            d = fn(junk, R[:, k, :], ACT.Sign, c, accum_out=sg0[:, it:it + 1])
            jtok = d
            ring_tok[k] = [b, d]
            st_r[it] = [a, b, c, d]

        t1_done = [None] * NT

        def evac1(it, b, tok):
            if Q.section is None and st_r[it] is None:
                row_stats(it)
            a = fn(tpart(S0, it), grid(bank(b)), ACT.Copy, tok, st_r[it][0] if Q.section is None else None,
                   scale=rmax[:, it:it + 1])
            t = stt(tpart(S1, it), grid(bank(b)), rmax[:, it:it + 1], tpart(S0, it), ALU.mult, ALU.subtract,
                    a, st_r[it][0] if Q.section is None else None)
            bfree[b] = [t]
            t1_done[it] = t

        none = Tasks()

        def first_product():
            for jt in range(NT):
                for it in range(8):
                    last[it] = pair(it, it, jt, rx(S0), rx(S1), p0[jt], bfree[it] if jt == 0 else None)
            for it in range(8):
                evac1(it, it, last[it])
            for it in range(8, NT):
                b = it - 8
                for jt in range(NT):
                    t = pair(b, it, jt, rx(S0), rx(S1), bfree[b] if jt == 0 else None)
                evac1(it, b, t)
            return t

        pe_t1 = first_product()

        d0 = tt(Wa[0:64, :], Wa[0:64, :], Wb[0:64, :], ALU.subtract, l_wa, l_wb)
        stc = lambda k, p=128: st[0:p, k:k + 1]
        w = [red(stc(0), Wa, ALU.max, d0, k_st, absolute=True),
             red(stc(1), Wb, ALU.max, absolute=True),
             red(stc(2), bds[:, 3, :], ALU.max, l_bd, absolute=True),
             red(stc(3), bds[:, 0:2, :].rearrange("p k m -> p (k m)"), ALU.max, absolute=True),
             red(stc(4), bds[:, 2, :], ALU.max, absolute=True),
             red(stc(5, 64), nrm[0:64, 0, :], ALU.add, l_w1n, absolute=True),
             red(stc(6, 64), nrm[0:64, 1, :], ALU.add, absolute=True),
             red(stc(7, 64), nrm[0:64, 2, :], ALU.add, l_w2n, absolute=True),
             red(stc(8), b1c[:, :], ALU.max, l_b1, absolute=True),
             red(stc(9), rows[:, 1, :], ALU.max, l_rows, absolute=True),
             red(stc(10), rows[:, 2, :], ALU.max, absolute=True)]
        ar1 = pool(lambda e: e.partition_all_reduce(sr[:, :], st[:, :], 128, bass.bass_isa.ReduceOp.max), w)

        (cS, cX, cG, cS0, cWL, cW1, cW2, cLam, cSmax, cE, cEb, cV1, cSX, cVl,
         cB0, cT) = range(16)
        cs_sv, cs_sh, cs_ch, cs_cv = 16, 20, 23, 26
        cTmp = 32
        one_of = lambda k: sr[:, k:k + 1]
        m0 = tt(col(cTmp), one_of(0), one_of(1), ALU.max, ar1)

        def recip_scale(dst, src, num, *w):
            a = ts(col(dst), src, 1e-30, 1.0 / num, ALU.max, ALU.mult, *w)
            return dve(lambda e: e.reciprocal(col(dst), col(dst)), a)

        q0 = recip_scale(cS0, col(cTmp), 1024.0, m0)
        q1 = recip_scale(cWL, one_of(2), 1024.0, ar1)
        q2 = recip_scale(cW1, one_of(3), 1024.0, ar1)
        q3 = recip_scale(cW2, one_of(4), 1024.0, ar1)

        def halves(hi, lo, src, c, *w):
            a = fn(hi, src, ACT.Copy, *w, scale=c)
            return stt(lo, src, c, hi, ALU.mult, ALU.subtract, a, *w)

        h0 = halves(W01[:, 0, :], W01[:, 1, :], Wa, col(cS0), q0)
        h1 = halves(W2[:, 0, :], W2[:, 1, :], Wb, col(cS0), q0)
        h2 = halves(bdh[:, 0:2, :], bdl[:, 0:2, :], bds[:, 0:2, :], col(cW1), q2)
        h3 = halves(bdh[:, 2, :], bdl[:, 2, :], bds[:, 2, :], col(cW2), q3)
        h4 = halves(bdh[:, 3, :], bdl[:, 3, :], bds[:, 3, :], col(cWL), q1)
        w_ready = [h0, h1, h2, h3, h4]

        allr = [t for x in st_r for t in x]
        a1 = stt(deg, sg1, float(N), rmax, ALU.add, ALU.mult, allr)
        a2 = stt(sg1, sg1, float(N), sg0, ALU.add, ALU.subtract, a1)
        f = [red(fl[:, 0:1], sg1, ALU.max, a2, absolute=True),
             dve(lambda e: e.tensor_reduce(fl[:, 1:2], rmin, op=ALU.min, axis=AX.X, negate=True), allr),
             red(fl[:, 2:3], rmax, ALU.max),
             red(fl[:, 3:4], deg, ALU.max),
             red(fl[:, 4:5], xm[:, :], ALU.max, mx)]
        ar2 = pool(lambda e: e.partition_all_reduce(fr[:, :], fl[:, :], 128, bass.bass_isa.ReduceOp.max), f)
        c1 = copy(DV, col(cS), fr[:, 3:4], ar2)
        c2 = copy(DV, col(cX), fr[:, 4:5])
        c3 = dve(lambda e: e.memset(col(cSX), SX))

        def span(dst, *w):
            a = tt(col(dst), col(cS), col(cS), ALU.mult, *w)
            b = ts(col(dst), col(dst), 2.0, 1.0, ALU.mult, ALU.max, a)
            return tt(col(dst), col(dst), col(cX), ALU.mult, b)

        c4 = span(cTmp + 1, c1, c2)
        g = [ts(cs[:, 40:41], fr[:, 0:1], 0.0, None, ALU.is_gt, None),
             ts(cs[:, 41:42], fr[:, 1:2], 0.0, None, ALU.is_gt, None),
             ts(cs[:, 42:43], fr[:, 3:4], 8.0, None, ALU.is_gt, None),
             ts(cs[:, 43:44], col(cTmp + 1), 1000.0, None, ALU.is_gt, None, c4),
             ts(cs[:, 44:45], fr[:, 4:5], 1.0 / 64, None, ALU.is_lt, None)]
        g1 = red(fi[:, 0:1], cs[:, 40:45], ALU.max, g)
        g2 = ts(fi[:, 1:2], fr[:, 2:3], 0.5, None, ALU.is_gt, None)
        flags = {}

        def load_flags(eng):
            def do(e):
                v = e.value_load(fi[0:1, 0:1])
                u = e.value_load(fi[0:1, 1:2])
                flags[eng, "G"] = lambda: v
                flags[eng, "H"] = lambda: u
                return e.nop()
            return Q.op(eng, do, g1, g2)

        for eng in ENGINES:
            load_flags(eng)

        Q.section = "G"
        gt = [None] * 2
        gtd = None
        for it in range(NT):
            k = it % 2
            ld = Q.load(SP, R[:, k, :], ar[it], s_gr[k], gt[k], gtd, pe_t1, g1)
            a = red(rmax[:, it:it + 1], R[:, k, :], ALU.max, ld, absolute=True)
            b = red(sg0[:, it:it + 1], R[:, k, :], ALU.add, absolute=True)
            c = red(deg[:, it:it + 1], R[:, k, :], ALU.add)
            gt[k] = c
        u = ts(rmax, rmax, 1e-30, 1.0 / 4096, ALU.max, ALU.mult, c)
        u = dve(lambda e: e.reciprocal(nr, rmax), u)
        u = red(fl[:, 3:4], sg0, ALU.max, u)
        u = pool(lambda e: e.partition_all_reduce(fr[:, :], fl[:, :], 128, bass.bass_isa.ReduceOp.max), u)
        u = copy(DV, col(cS), fr[:, 3:4], u)
        u = span(cTmp + 1, u)
        u = recip_scale(cSX, col(cTmp + 1), 8192.0, u)
        for jt in range(NT):
            u = split(jt, col(cSX), u, pe_t1)
        for it in range(NT):
            dg = M2[:, 0:128]
            u = ts(dg, i32[:, :], nr[:, it:it + 1], None, ALU.mult, None, u, k_i32, jtok)
            o = PS[:, (it % 16) * 128:(it % 16) * 128 + 128]
            u = mm(o, ones[:, :], dg, True, True, u, k_one, [bfree[x] for x in range(8)])
        u = copy(DV, R[:, 2, :], PS[:, 0:2048], u)
        qrow = R[:, 2, :]
        gx = u
        gw = [None, None]
        at_t = R[:, 1, :]
        lo_t = M2[:, 0:1024].bitcast(F16)
        for jt in range(NT):
            ld = Q.load(SP, R[:, 0, :], atr[jt], s_gr[2], u)
            a = tt(at_t, R[:, 0, :], qrow, ALU.mult, ld, u)
            b = copy(DV, Bm[:, jt, :], at_t, a)
            c = tt(lo_t, at_t, Bm[:, jt, :], ALU.subtract, b, gw[0])
            gw[0] = Q.load(SP, blo[:, :, jt, :].rearrange("t p i -> p t i"),
                           lo_t.rearrange("p (t i) -> p t i", i=128), s_gw, c)
            u = c
        gload["saved"] = [gw[0], u]

        ev = None
        for it in range(NT):
            b = it % 8
            for jt in range(NT):
                if jt == NT - 1:
                    low_pass([it], [b], rx(S0), u)
                t = pair(b, it, jt, rx(S0), rx(S1), u, gx, t1_done[it - 8] if it >= 8 else None)
            evac1(it, b, t)
        gdve = t1_done[NT - 1]
        dve(lambda e: e.nop(), gdve)
        act(lambda e: e.nop(), gdve)
        Q.section = None
        fence = dve(lambda e: e.nop())
        for k in range(NT):
            t1_done[k] = fence
        for k in range(8):
            bfree[k] = [fence]

        u = tt(col(cE), col(cSX), col(cS0), ALU.mult, c1, c2, c3, q0)
        u = dve(lambda e: e.reciprocal(col(cE), col(cE)), u)
        e_emb = dve(lambda e: e.tensor_scalar(emb[:, :, :], emb[:, :, :], col(cE), None, ALU.mult), u, l_emb)
        e_r2 = ts(r2, rmax, 2.0, None, ALU.mult, None)
        u = ts(col(cTmp), col(cS), 1.0, 1.0 / 2048, ALU.add, ALU.mult)
        lam = dve(lambda e: e.reciprocal(col(cLam), col(cTmp)), u)
        u = tt(col(cEb), col(cLam), col(cLam), ALU.mult, lam)
        e_epsL = ts(col(cEb), col(cEb), 1e-5, None, ALU.mult, None, u)
        u = tt(col(cTmp), col(cLam), col(cLam), ALU.mult)
        u = dve(lambda e: e.reciprocal(col(cTmp), col(cTmp)), u)
        n_in1 = [ts(col(45), col(cTmp), 1.0 / C, None, ALU.mult, None, u),
                 ts(col(46), col(cTmp), 1e-5, None, ALU.mult, None),
                 ts(col(47), col(cTmp), 0.0, 1.0 / C, ALU.mult, ALU.add),
                 ts(col(48), col(cTmp), 0.0, 1e-5, ALU.mult, ALU.add)]
        LN_11 = (col(47), col(48))
        LN_1L = (col(45), col(46))
        LN_LL = (col(47), col(48))
        LN_LL = (col(45), col(48))
        LN_L1 = (col(47), col(cEb))
        u = ts(deg, deg, 1.0, None, ALU.add, None)
        u = ts(cw, deg, col(cWL), None, ALU.mult, None, u, q1)
        e_cw = dve(lambda e: e.reciprocal(cw, cw), u)
        e_lb = ts(b2s[:, 3, :], rows[:, 0, :], col(cLam), None, ALU.mult, None, lam)
        u = ts(col(cSmax), col(cS), 1.0, None, ALU.max, None)

        def v_scale(t, v, *w):
            a = tt(col(50 + t), v, col(cSmax), ALU.mult, *w)
            a = ts(col(50 + t), col(50 + t), 1e-30, 1.0 / 32768, ALU.max, ALU.mult, a)
            return dve(lambda e: e.reciprocal(col(cs_sv + t), col(50 + t)), a)

        def step_scales(t, v, *w):
            c = tt(col(35), one_of(6), col(cS), ALU.mult, *w)
            c = tt(col(35), col(35), one_of(5), ALU.add, c)
            c = tt(col(35), col(35), v, ALU.mult, c)
            c = tt(col(35), col(35), one_of(8), ALU.add, c)
            d = recip_scale(cs_sh + t, col(35), 32768.0, c)
            f1 = tt(col(36), col(cs_sv + t), col(cW1), ALU.mult, d)
            f1 = dve(lambda e: e.reciprocal(col(36), col(36)), f1)
            f1 = tt(col(cs_ch + t), col(36), col(cs_sh + t), ALU.mult, f1)
            f2 = tt(b1s[:, t:t + 1], b1c[:, :], col(cs_sh + t), ALU.mult)
            g3 = tt(col(38), col(cs_sh + t), col(cW2), ALU.mult)
            g3 = dve(lambda e: e.reciprocal(col(38), col(38)), g3)
            if t < 2:
                g4 = tt(col(37), one_of(7), col(35), ALU.mult)
                g4 = tt(col(33), col(37), one_of(9), ALU.add, g4)
                g4 = v_scale(t + 1, col(33), g4)
                by = col(cs_sv + t + 1)
            else:
                by, g4 = col(cLam), None
            k5 = tt(col(cs_cv + t), col(38), by, ALU.mult, g3, g4)
            k6 = ts(b2s[:, t, :], rows[:, 1, :], by, None, ALU.mult, None, g4)
            return [f1, f2, k5, k6]

        v0 = ts(col(32), one_of(10), 8.0, None, ALU.max, None, u)
        v0 = v_scale(0, col(32), v0)
        step_tok = {0: step_scales(0, col(32), v0)}
        scal = list(step_tok[0])
        u = dve(lambda e: e.reciprocal(col(39), col(cLam)))
        k_v0 = tt(col(cV1), col(cs_sv), col(39), ALU.mult, u)
        u = dve(lambda e: e.tensor_copy(rows[0:1, 2, :], rows[0:1, 2, :]))
        scal += [k_v0, u, e_lb, e_cw, lam, e_epsL] + n_in1
        scales_done = scal[-1]

        nln = [0]
        sq_free = [None, None]

        def layernorm(it, y, cols, dst=None):
            slot = nln[0] % 2
            nln[0] += 1
            sq = M2[:, 1024 + slot * 512:1536 + slot * 512]
            s = sm[:, slot, :]
            xt = X[:, it, :]
            a = red(s[:, 0:8], grid(xt), ALU.add, y, sq_free[slot])
            a = ts(s[:, 8:16], s[:, 0:8], -1.0 / C, None, ALU.mult, None, a)
            xc = tt(grid(xt), grid(xt), spread(s[:, 8:16]), ALU.add, a)
            a = fn(sq, xt, ACT.Square, xc, sq_free[slot])
            yield None
            b = red(s[:, 0:8], grid(sq), ALU.add, a)
            b = ts(s[:, 16:24], s[:, 0:8], cols[0], cols[1], ALU.mult, ALU.add, b, scales_done)
            b = fn(s[:, 24:32], s[:, 16:24], ACT.Sqrt, b)
            yield None
            b = dve(lambda e: e.reciprocal(s[:, 24:32], s[:, 24:32]), b)
            c = tt(s[:, 0:8], s[:, 24:32], s[:, 24:32], ALU.mult, b)
            c = tt(s[:, 0:8], s[:, 0:8], s[:, 16:24], ALU.mult, c)
            c = ts(s[:, 0:8], s[:, 0:8], -0.5, 1.5, ALU.mult, ALU.add, c)
            b = tt(s[:, 16:24], s[:, 24:32], s[:, 0:8], ALU.mult, c)
            o = X[:, it, :] if dst is None else dst
            t = tt(grid(o), grid(xt), spread(s[:, 16:24]), ALU.mult, b)
            sq_free[slot] = t
            yield t

        def run(gen):
            for t in gen:
                pass
            return t

        TA = T3[:, :].bitcast(F16).rearrange("p (g k n) -> p g k n", k=8, n=128)
        ta_free = [c_nb, c_nb]
        nb_all = []
        for it in range(NT):
            nb_all.append(tt(grid(X[:, it, :]), grid(X[:, it, :]), each_b(NB[:, it, :]), ALU.add,
                             c_nb, fence, on=PO))
        ta_free = [[nb_all[-1], h0, h1], [nb_all[-1], h0, h1]]
        xsum = M2[:, 512:1024]
        erow = M2[:, 0:512]
        z = pool(lambda e: e.memset(xsum, 0.0), jtok, fence)
        xs_tok = [z]
        l0_done = [None] * NT
        t2n = [0]
        tfree = [None, None]
        tb = [2, 3]
        tbi = [0]
        ei = [0]
        done0 = [None] * NT

        def work0(it, t2a, slot):
            T2 = R[:, 0, :].bitcast(F16)[:, slot * 1024:(slot + 1) * 1024]
            g3 = TA[:, 3 * slot:3 * slot + 3]
            ok = []
            for g, (src, w1) in enumerate(((S0[:, it, :], None), (S1[:, it, :], None), (T2, t2a))):
                b = tb[tbi[0] % 2]
                tbi[0] += 1
                for k in range(B):
                    t = transpose(bank16(b)[:, k * 128:(k + 1) * 128], src[:, k * 128:(k + 1) * 128], i16[:, :],
                                  bfree[b], w1, k_i16, t1_done[it])
                c = copy(AC if g != 1 else DV, g3[:, g, :, :].rearrange("p k n -> p (k n)"), bank16(b), t,
                         ta_free[slot])
                bfree[b] = [c]
                ok.append(c)
                if g == 2:
                    tfree[slot] = t
            yield
            y = nb_all[it]
            for g in range(2):
                for bp in range(4):
                    b0 = 4 + 2 * (ei[0] % 2)
                    ei[0] += 1
                    for j in range(2):
                        b, k = b0 + j, 2 * bp + j
                        fr_ = bfree[b]
                        wc = slice(g * 512, (g + 1) * 512)
                        mm(bank(b), g3[:, 0, k, :], W01[:, 0, wc], True, False, fr_, ok, w_ready)
                        mm(bank(b), g3[:, 0, k, :], W01[:, 1, wc], False, False)
                        mm(bank(b), g3[:, 1, k, :], W01[:, 0, wc], False, False)
                        mm(bank(b), g3[:, 2, k, :], W2[:, 0, wc], False, False)
                        t = mm(bank(b), g3[0:64, 2, k, :], W2[0:64, 1, wc], False, True)
                    ps = PS[:, b0 * 512:(b0 + 2) * 512].rearrange("p (b d o) -> p b d o", b=2, o=C)
                    xv = X[:, it, bp * 128:(bp + 1) * 128].rearrange("p (b o) -> p b o", o=C)
                    for d in range(8):
                        y = stt(xv, ps[:, :, d, :], emb[:, it, g * 8 + d:g * 8 + d + 1], xv, ALU.mult, ALU.add,
                                t, y, e_emb)
                    bfree[b0] = [y]
                    bfree[b0 + 1] = [y]
                    if (g, bp) == (1, 3):
                        ta_free[slot] = t
                    yield
            gen = layernorm(it, y, LN_11)
            for t in gen:
                if t is None:
                    yield
            done0[it] = t
            xs_tok[0] = tt(xsum, xsum, X[:, it, :], ALU.add, t, xs_tok[0], on=PO)

        tasks = Tasks(width=2)
        cnt0 = [0]

        def evac2(it, b, tok):
            slot = cnt0[0] % 2
            cnt0[0] += 1
            T2 = R[:, 0, :].bitcast(F16)[:, slot * 1024:(slot + 1) * 1024].rearrange(
                "p (b k c) -> p b k c", k=2, c=C)
            a = fn(T2[:, :, 0, :], grid(bank(b)), ACT.Copy, tok, tfree[slot], e_r2, ring_tok,
                   scale=r2[:, it:it + 1])
            t = stt(T2[:, :, 1, :], grid(bank(b)), r2[:, it:it + 1], T2[:, :, 0, :], ALU.mult, ALU.subtract,
                    a, e_r2)
            bfree[b] = [t]
            tasks.add(work0(it, t, slot))

        def rt(S):
            return lambda jt: tpart(S, jt)

        tasks = Tasks(width=1)
        nmm = 0
        order = list(range(NT))
        for jt in range(NT):
            if jt == NT - 1:
                low_pass([0, 1], [0, 1], rt(S0), t1_done)
            for it in (0, 1):
                last[it] = pair(it, it, jt, rt(S0), rt(S1), t1_done[jt], bfree[it] if jt == 0 else None)
        evac2(0, 0, last[0])
        evac2(1, 1, last[1])
        tasks.slot()
        for it in range(2, NT):
            b = it % 2
            for jt in range(NT):
                if jt == NT - 1:
                    low_pass([it], [b], rt(S0))
                t = pair(b, it, jt, rt(S0), rt(S1), bfree[b] if jt == 0 else None)
                if jt % 2 == 1:
                    tasks.slot()
            tasks.until(lambda: len(tasks.wait) < 2 and (len(tasks.wait) < 1 or done0[it - 2] is not None))
            tasks.until(lambda: done0[it - 2] is not None)
            tasks.slot()
            evac2(it, b, t)
        while tasks.slot():
            pass

        mm_s = mm(bank(0), ones[:, :], xsum, True, True, xs_tok[0], bfree[0], k_one)
        a = ts(erow, bank(0), 1.0 / N, 0.0, ALU.mult, ALU.min, mm_s, jtok)
        b = fn(M2[:, 1024:1536], erow, ACT.Exp, a, sq_free)
        a = ts(erow, bank(0), 1.0 / N, 0.0, ALU.mult, ALU.max, b, a)
        bfree[0] = [a]
        k_er = stt(erow, M2[:, 1024:1536], -1.0, erow, ALU.add, ALU.add, a, b)
        sq_free = [k_er, k_er]
        l0_all = list(done0)

        Q.section = "H"
        sc = S0[:, :, :].rearrange("p t n -> p (t n)").bitcast(F32)
        hA, hrow, hU, hM = (sc[:, k * 2048:(k + 1) * 2048] for k in range(4))
        hP, hPT = R[:, 0, :], R[:, 1, :]
        E = S1[:, :, :].rearrange("p t n -> p (t n)").bitcast(F32).rearrange("p (t n) -> p t n", t=NT)
        s12 = W01[:, :, :].rearrange("p a n -> p (a n)").bitcast(F32)[:, 0:256].rearrange(
            "p (k t b) -> p k t b", k=2, b=B)
        u = [k_er, l0_all, h0]
        for it in range(NT):
            for k in range(2):
                u = tt(grid(hU[:, 0:512]), grid(X[:, it, :]), each_b(rows[:, 3 + k, :]), ALU.mult, u)
                u = red(s12[:, k, it, :], grid(hU[:, 0:512]), ALU.add, u)
        hb = bfree
        small8 = W01[:, 1, :].bitcast(F32)
        for b in range(B):
            for it in range(NT):
                u = ts(hP[:, 0:128], i32[:, :], s12[:, 1, it, b:b + 1], None, ALU.mult, None, u)
                u = mm(PS[:, it * 128:(it + 1) * 128], ones[:, :], hP[:, 0:128], True, True, u,
                       [bfree[x] for x in range(8)])
            u = copy(DV, hrow, PS[:, 0:2048], u)
            for it in range(NT):
                ld = Q.load(SP, hA, ar[it], s_h, u)
                a = ts(hU, hrow, s12[:, 0, it, b:b + 1], None, ALU.add, None, u)
                a = stt(hU, hU, 0.2, hU, ALU.mult, ALU.max, a)
                m = ts(hM, hA, 0.5, None, ALU.is_gt, None, ld, a)
                a = tt(hU, hU, hM, ALU.mult, m)
                m = ts(hM, hM, 1.0, 9000000000000000.0, ALU.subtract, ALU.mult, a)
                a = tt(hU, hU, hM, ALU.add, m)
                a = dve(lambda e: e.tensor_reduce(small8[:, 0:1], hU, op=ALU.max, axis=AX.X, negate=True), a)
                a = fn(hP, hU, ACT.Exp, a, bias=small8[:, 0:1], accum_out=small8[:, 1:2])
                for jt in range(NT):
                    t = transpose(PS[:, jt * 128:(jt + 1) * 128], hP[:, jt * 128:(jt + 1) * 128], i32[:, :], a)
                c = copy(DV, hPT, PS[:, 0:2048], t)
                for jt in range(NT):
                    t = mm(PS[:, 2048:2112], hPT[:, jt * 128:(jt + 1) * 128], X[:, jt, b * C:(b + 1) * C],
                           jt == 0, jt == NT - 1, c)
                d = dve(lambda e: e.reciprocal(small8[:, 2:3], small8[:, 1:2]), t)
                d = ts(small8[:, 64:128], PS[:, 2048:2112], small8[:, 2:3], 0.0, ALU.mult, ALU.min, d)
                f3 = fn(small8[:, 128:192], small8[:, 64:128], ACT.Exp, d)
                d = ts(small8[:, 64:128], PS[:, 2048:2112], small8[:, 2:3], 0.0, ALU.mult, ALU.max, f3)
                u = stt(E[:, it, b * C:(b + 1) * C], small8[:, 128:192], -1.0, small8[:, 64:128],
                        ALU.add, ALU.add, d)
        for it in range(NT):
            u = tt(X[:, it, :], X[:, it, :], E[:, it, :], ALU.add, u)
        u = ts(erow, erow, 0.0, None, ALU.mult, None, u)
        dve(lambda e: e.nop(), u)
        Q.section = None
        fence = dve(lambda e: e.nop())
        for k in range(8):
            bfree[k] = bfree[k] + [fence]

        sets = []
        for S in (S0, S1):
            v = S[:, :, :].rearrange("p t n -> p (t n)").rearrange("p (k t n) -> p k t n", k=2, n=BC)
            sets.append((v[:, 0], v[:, 1]))
        ready = [[None] * NT for _ in range(6)]
        tmp_free = {}

        tasks = Tasks(width=2)
        xready = [None] * NT

        def work1(it):
            y = tt(X[:, it, :], X[:, it, :], erow, ALU.add, k_er, fence)
            for t in layernorm(it, y, LN_1L):
                if t is None:
                    yield
            H, L = sets[0]
            a = copy(AC, H[:, it, :], X[:, it, :], t)
            b = tt(L[:, it, :], X[:, it, :], H[:, it, :], ALU.subtract, a, on=PO)
            xready[it] = t
            ready[0][it] = [a, b]
            yield

        for it in range(NT):
            tasks.add(work1(it))

        def region(k):
            pieces = [T3[:, i * 512:(i + 1) * 512] for i in range(6)]
            w = [W01[:, i, :].bitcast(F32) for i in range(2)] + [W2[:, i, :].bitcast(F32) for i in range(2)]
            r = [R[:, 1, i * 512:(i + 1) * 512] for i in range(4)] + [R[:, 0, i * 512:(i + 1) * 512] for i in range(4)]
            return (pieces + w + r)[k]

        def halves_of(k):
            v = region(k).bitcast(F16)
            return v[:, 0:512], v[:, 512:1024]

        taux = [4, 5, 6, 7]
        nx = [0]

        def aux():
            b = taux[nx[0] % len(taux)]
            nx[0] += 1
            return b

        free = {}

        def transposed(dst, src, on, w):
            b = aux()
            for k in range(8):
                t = transpose(bank16(b)[:, k * 128:(k + 1) * 128], src[k], i16[:, :], bfree[b], w)
            c = copy(on, dst, bank16(b), t, free.get(id(dst)))
            bfree[b] = [c]
            return c, t

        ring_use = {}

        def take(k):
            return ring_use.get(k)

        def work2(it, b, tok, slot):
            k0 = 5 * slot
            z = region(k0)
            zh, zl = halves_of(k0 + 1)
            zt = region(k0 + 2).bitcast(F16)
            a = stt(z, bank(b), rmax[:, it:it + 1], X[:, it, :], ALU.mult, ALU.add, tok, xready[it],
                    take(k0), fence)
            bfree[b] = [a]
            unread[b] = False
            p = copy(AC, zh, z, a, take(k0 + 1))
            q = tt(zl, z, zh, ALU.subtract, p, on=PO)
            xb = tt(grid(X[:, it, :]), grid(X[:, it, :]), each_b(b2s[:, 3, :]), ALU.add, a, on=PO)
            ring_use[k0] = [p, q]
            yield
            ab = aux()
            for k in range(8):
                src = (zh, zl)[k // 4][:, (k % 4) * 128:(k % 4 + 1) * 128]
                t = transpose(bank16(ab)[:, k * 128:(k + 1) * 128], src, i16[:, :], bfree[ab], p, q)
            ring_use[k0 + 1] = t
            c = copy(AC, zt, bank16(ab), t, take(k0 + 2))
            bfree[ab] = [c]
            yield
            ab = aux()
            for k in range(4):
                o = bank(ab)[:, k * 128:(k + 1) * 128]
                lh, ll = zt[:, k * 128:(k + 1) * 128], zt[:, (k + 4) * 128:(k + 5) * 128]
                mm(o, lh, bdh[:, 3, :], True, False, bfree[ab], c, w_ready)
                mm(o, lh, bdl[:, 3, :], False, False)
                t = mm(o, ll, bdh[:, 3, :], False, True)
            ring_use[k0 + 2] = t
            y = stt(X[:, it, :], bank(ab), cw[:, it:it + 1], X[:, it, :], ALU.mult, ALU.add, t, xb, e_cw)
            bfree[ab] = [y]
            yield
            for t in layernorm(it, y, LN_LL):
                if t is None:
                    yield
            xready[it] = t
            H, L = sets[1]
            src = X[:, it, :]
            w = t
            if it == 0:
                src = R[:, 0, 1536:2048]
                w = copy(PO, src, X[:, 0, :], t, scales_done)
                v = ts(grid(src[0:1, :]), rows[0:1, 2:3, :].broadcast_to([1, B, C]), col(cLam)[0:1, :], None,
                       ALU.mult, None, w)
                w = v
            p = fn(H[:, it, :], src, ACT.Copy, w, scale=col(cV1))
            q = stt(L[:, it, :], src, col(cV1), H[:, it, :], ALU.mult, ALU.subtract, p)
            ready[1][it] = [p, q]
            yield

        def rs(S):
            return lambda jt: S[:, jt, :]

        slots = [0]
        prev = {"tasks": tasks}

        def next_evac(work):
            def evac(it, b, tok):
                unread[b] = True
                s = slots[0] % 2
                slots[0] += 1
                tasks.add(work(it, b, tok, s))
            return evac

        product([0, 1, 2, 3], list(range(4, NT)), [0, 1, 2, 3], rs(sets[0][0]), rs(sets[0][1]),
                lambda jt: ready[0][jt], next_evac(work2), tasks)

        outs = []
        orr = out.rearrange("b (t p) c -> t p b c", p=128)

        def make3(t):
            H0, L0 = sets[(t + 1) % 2]
            H1, L1 = sets[t % 2]

            def work3(it, b, tok, slot):
                k0 = 6 * slot
                eh, el = halves_of(k0)
                et = region(k0 + 1).bitcast(F16)
                vt = region(k0 + 2).bitcast(F16)
                hh = region(k0 + 3)
                h16, hl16 = halves_of(k0 + 4)
                vv = region(k0 + 5)
                a = fn(eh, bank(b), ACT.Copy, tok, take(k0), fence, scale=rmax[:, it:it + 1])
                q = stt(el, bank(b), rmax[:, it:it + 1], eh, ALU.mult, ALU.subtract, a)
                bfree[b] = [q]
                unread[b] = False
                if t == 2:
                    xb = tt(grid(X[:, it, :]), grid(X[:, it, :]), each_b(b2s[:, 2, :]), ALU.add,
                            xready[it], step_tok[t], on=PO)
                ab = aux()
                for k in range(8):
                    src = (H0, L0)[k // 4][:, it, (k % 4) * 128:(k % 4 + 1) * 128]
                    tv = transpose(bank16(ab)[:, k * 128:(k + 1) * 128], src, i16[:, :], bfree[ab],
                                   ready[1 + t][it])
                cv = copy(AC, vt, bank16(ab), tv, take(k0 + 2))
                bfree[ab] = [cv]
                yield
                ab = aux()
                for k in range(8):
                    src = (eh, el)[k // 4][:, (k % 4) * 128:(k % 4 + 1) * 128]
                    te = transpose(bank16(ab)[:, k * 128:(k + 1) * 128], src, i16[:, :], bfree[ab], q)
                ring_use[k0] = te
                ce = copy(DV, et, bank16(ab), te, take(k0 + 1))
                bfree[ab] = [ce]
                yield
                ab = aux()
                for k in range(4):
                    o = bank(ab)[:, k * 128:(k + 1) * 128]
                    vh, vl = vt[:, k * 128:(k + 1) * 128], vt[:, (k + 4) * 128:(k + 5) * 128]
                    ehh, ell = et[:, k * 128:(k + 1) * 128], et[:, (k + 4) * 128:(k + 5) * 128]
                    mm(o, bdh[:, 0, :], vh, True, False, bfree[ab], ce, cv, w_ready)
                    mm(o, bdh[:, 0, :], vl, False, False)
                    mm(o, bdl[:, 0, :], vh, False, False)
                    mm(o, bdh[:, 1, :], ehh, False, False)
                    mm(o, bdh[:, 1, :], ell, False, False)
                    m = mm(o, bdl[:, 1, :], ehh, False, True)
                ring_use[k0 + 1] = m
                ring_use[k0 + 2] = m
                r = fn(hh, bank(ab), ACT.Relu, m, take(k0 + 3), step_tok[t],
                       scale=col(cs_ch + t), bias=b1s[:, t:t + 1])
                bfree[ab] = [r]
                p = copy(DV, h16, hh, r, take(k0 + 4))
                q = tt(hl16, hh, h16, ALU.subtract, p, on=PO)
                ring_use[k0 + 3] = q
                yield
                ab = aux()
                for k in range(4):
                    o = bank(ab)[:, k * 128:(k + 1) * 128]
                    lh, ll = h16[:, k * 128:(k + 1) * 128], hl16[:, k * 128:(k + 1) * 128]
                    mm(o, lh, bdh[:, 2, :], True, False, bfree[ab], p, q)
                    mm(o, lh, bdl[:, 2, :], False, False)
                    m = mm(o, ll, bdh[:, 2, :], False, True)
                ring_use[k0 + 4] = m
                if t < 2:
                    v = stt(grid(vv), grid(bank(ab)), col(cs_cv + t), each_b(b2s[:, t, :]), ALU.mult, ALU.add,
                            m, take(k0 + 5), step_tok[t])
                    bfree[ab] = [v]
                    p = copy(AC, H1[:, it, :], vv, v)
                    vm[it] = red(vmx[:, it:it + 1], vv, ALU.max, v, absolute=True)
                    q = tt(L1[:, it, :], vv, H1[:, it, :], ALU.subtract, p, on=PO)
                    ring_use[k0 + 5] = [q, vm[it]]
                    ready[2 + t][it] = [p, q]
                    yield
                else:
                    y = stt(X[:, it, :], bank(ab), col(cs_cv + t), X[:, it, :], ALU.mult, ALU.add, m, xb)
                    bfree[ab] = [y]
                    yield
                    for tk in layernorm(it, y, LN_L1):
                        if tk is None:
                            yield
                    outs.append(Q.load(SP, orr[it], grid(X[:, it, :]), s_out[len(outs) % 2],
                                       tk, outs[-2] if len(outs) >= 2 else None))
                    yield
            return work3

        def measure(t):
            def mid():
                a = red(fl[:, 0:1], vmx[:, :], ALU.max, vm)
                b = pool(lambda e: e.partition_all_reduce(fr[:, 0:1], fl[:, 0:1], 128,
                                                          bass.bass_isa.ReduceOp.max), a)
                c = tt(col(32), fr[:, 0:1], col(50 + t), ALU.mult, b)
                step_tok[t] = step_scales(t, col(32), c)
            return mid

        for t in range(3):
            Hs, Ls = sets[(t + 1) % 2]
            product([0, 1, 2, 3], list(range(4, NT)), [0, 1, 2, 3], rs(Hs), rs(Ls),
                    lambda jt, t=t: ready[1 + t][jt], next_evac(make3(t)), tasks,
                    mid=measure(t) if t else None)
        while tasks.slot():
            pass
        Q.op(SP, lambda e: e.nop(), outs[-2:])

        Q.number()
        block = ctx.enter_context(nc.Block())

        @block.tensor
        def _(e):
            Q.replay(PE, e, flags)

        @block.vector
        def _(e):
            Q.replay(DV, e, flags)

        @block.scalar
        def _(e):
            Q.replay(AC, e, flags)

        @block.gpsimd
        def _(e):
            Q.replay(PO, e, flags)

        @block.sync
        def _(e):
            Q.replay(SP, e, flags)


_OUTS = [((8, 2048, 64), "float32")]


def kernel(**inputs):
    import concourse.bacc as _bacc
    from concourse.bass_utils import run_bass_kernel_spmd as _run

    def arr(name):
        return np.asarray(inputs[name])

    x, adj = arr("x"), arr("adj")
    emb, w0 = arr("L0_gnn_embedding"), arr("L0_gnn_weight")
    w1 = arr("L3_gnn_W1")
    rows = np.stack([arr("L2_gnn_b"), arr("L3_gnn_b2"), arr("L3_gnn_intervention_value")[0],
                     arr("L1_gnn_a")[:64, 0], arr("L1_gnn_a")[64:, 0]])
    b1 = arr("L3_gnn_b1")
    host = {
        "x_in": x.transpose(1, 0, 2).reshape(2048, 512),
        "at_in": adj.T,
        "a_in": adj,
        "embt_in": emb.T,
        "emb_in": emb,
        "w0_in": w0.transpose(1, 2, 0, 3).reshape(192, 1024),
        "w0b_in": arr("L0_gnn_bias"),
        "wl_in": arr("L2_gnn_W").T,
        "w1t_in": w1.T,
        "w2t_in": arr("L3_gnn_W2").T,
        "w1_in": w1,
        "w2_in": arr("L3_gnn_W2"),
        "b1_in": np.concatenate([b1, b1]).reshape(128, 1),
        "rows_in": np.tile(rows.reshape(1, 320), (128, 1)),
    }
    nc = _bacc.Bacc("TRN2", target_bir_lowering=False, num_devices=1, dynamic_dma_scratch_size=1024)
    arrays, args = {}, []
    for name, a in host.items():
        a = np.ascontiguousarray(a)
        arrays[name] = a
        args.append(nc.dram_tensor(name, a.shape, mybir.dt.from_np(a.dtype), kind="ExternalInput").ap())
    o = nc.dram_tensor("out_0", _OUTS[0][0], F32, kind="ExternalOutput").ap()
    gnn_kernel(nc, *args, o)
    r = _run(nc, [arrays], core_ids=[0])
    return r.results[0]["out_0"]
```

```python
import numpy as np
import concourse.bass as bass
from concourse import mybir
from contextlib import ExitStack

F32 = mybir.dt.float32
F16 = mybir.dt.float16
I32 = mybir.dt.int32
ALU = mybir.AluOpType
ACT = mybir.ActivationFunctionType
AX = mybir.AxisListType

NT = 16
B, C, D = 8, 64, 16
BC = B * C
N = 2048
PE, AC, DV, PO, SP = "tensor", "scalar", "vector", "gpsimd", "sync"
ENGINES = (PE, AC, DV, PO, SP)


class Tok:

    def __init__(self, section, sem=None, val=0):
        self.section, self.sem, self.val, self.used = section, sem, val, False


def tokens(waits):
    for w in waits:
        if isinstance(w, (list, tuple)):
            yield from tokens(w)
        elif w is not None:
            yield w


class Queues:

    def __init__(self, sems):
        self.q = {e: [] for e in ENGINES}
        self.sems = sems
        self.section = None
        self.dma = {}

    def op(self, eng, fn, *waits):
        tok = Tok(self.section)
        flat = list(tokens(waits))
        for w in flat:
            assert w.section is None or w.section == self.section, "a wait on what may not run"
            w.used = True
        self.q[eng].append((self.section, fn, flat, tok))
        return tok

    def load(self, eng, out, in_, sem, *waits):
        tok = Tok(self.section, sem, self.dma.get(id(sem), 0) + 16)
        self.dma[id(sem)] = tok.val
        self.op(eng, lambda e: (e.dma_start(out, in_).then_inc(sem, 16), None)[1], *waits)
        return tok

    def number(self):
        for eng in ENGINES:
            count = {}
            for section, _, _, tok in self.q[eng]:
                if tok.used and tok.sem is None:
                    count[section] = count.get(section, 0) + 1
                    tok.sem, tok.val = self.sems[eng, section], count[section]

    def replay(self, eng, e, flags):
        seen = {}
        items, k = self.q[eng], 0

        def emit(item, seen):
            _, fn, waits, tok = item
            need = {}
            for w in waits:
                if seen.get(id(w.sem), 0) < w.val:
                    need[id(w.sem)] = (w.sem, max(w.val, need.get(id(w.sem), (0, 0))[1]))
            for key, (sem, val) in need.items():
                e.wait_ge(sem, val)
                seen[key] = val
            ins = fn(e)
            if tok.used:
                ins.then_inc(tok.sem, 1)

        while k < len(items):
            section = items[k][0]
            end = k
            while end < len(items) and items[end][0] == section:
                end += 1
            if section is None:
                for item in items[k:end]:
                    emit(item, seen)
            else:
                with e.If(flags[eng, section]()):
                    inner = dict(seen)
                    for item in items[k:end]:
                        emit(item, inner)
            k = end


def gnn_kernel(nc, x_in, at_in, a_in, embt_in, emb_in, w0_in, w0b_in, wl_in, w1t_in, w2t_in,
               w1_in, w2_in, b1_in, rows_in, out):
    ctx = ExitStack()
    with ctx:
        def sb(name, shape, dt):
            return ctx.enter_context(nc.sbuf_tensor(name, shape, dt))

        def sem(name):
            return ctx.enter_context(nc.semaphore(name))

        Bm = sb("Bm", [128, NT, N], F16)
        S0 = sb("S0", [128, NT, 1024], F16)
        S1 = sb("S1", [128, NT, 1024], F16)
        X = sb("X", [128, NT, BC], F32)
        R = sb("R", [128, 3, N], F32)
        W01 = sb("W01", [128, 2, 1024], F16)
        W2 = sb("W2", [128, 2, 1024], F16)
        T3 = sb("T3", [128, 3072], F32)
        M2 = sb("M2", [128, 2048], F32)
        bdh = sb("bdh", [128, 4, 128], F16)
        bdl = sb("bdl", [128, 4, 128], F16)
        i16 = sb("i16", [128, 128], F16)
        i32 = sb("i32", [128, 128], F32)
        ones = sb("ones", [128, 128], F32)
        emb = sb("emb", [128, NT, D], F32)
        rows = sb("rows", [128, 5, C], F32)
        b1c = sb("b1c", [128, 1], F32)
        b1s = sb("b1s", [128, 3], F32)
        b2s = sb("b2s", [128, 4, C], F32)
        nrm = sb("nrm", [128, 3, C], F32)
        st = sb("st", [128, 12], F32)
        sr = sb("sr", [128, 12], F32)
        fl = sb("fl", [128, 5], F32)
        fr = sb("fr", [128, 5], F32)
        fi = sb("fi", [128, 2], I32)
        cs = sb("cs", [128, 64], F32)
        ra = sb("ra", [128, 8, NT], F32)
        xm = sb("xm", [128, NT], F32)
        sm = sb("sm", [128, 3, 64], F32)
        PS = ctx.enter_context(nc.psum_tensor("PS", [128, 4096], F32))

        blo = nc.dram_tensor("blo", [NT, 128, NT, 128], F16, kind="Internal").ap()

        vmx = sb("vmx", [128, NT], F32)
        vm = [None] * NT
        rmax, cnt, nr, sg1, sg0, deg, r2, cw = (ra[:, k, :] for k in range(8))

        def bank(b):
            return PS[:, b * 512:(b + 1) * 512]

        def bank16(b):
            return bank(b).bitcast(F16)

        def col(k):
            return cs[:, k:k + 1]

        def grid(ap, n=C):
            return ap.rearrange("p (b c) -> p b c", c=n)

        def spread(ap8):
            return ap8.unsqueeze(2).broadcast_to([128, B, C])

        def each_b(ap64):
            return ap64.unsqueeze(1).broadcast_to([128, B, C])

        sems = {(e, s): sem(f"s_{e}_{s}") for e in ENGINES for s in (None, "G", "H")}
        Q = Queues(sems)
        s_ring = [sem(f"s_ring{k}") for k in range(3)]
        s_x = [sem(f"s_x{k}") for k in range(NT)]
        s_small = [sem(f"s_small{k}") for k in range(20)]
        s_gr = [sem(f"s_gr{k}") for k in range(3)]
        s_gw = sem("s_gw")
        s_gb = [sem(f"s_gb{k}") for k in range(2)]
        s_h = sem("s_h")
        s_out = [sem(f"s_out{k}") for k in range(2)]

        def pe(fn, *w): return Q.op(PE, fn, *w)
        def act(fn, *w): return Q.op(AC, fn, *w)
        def dve(fn, *w): return Q.op(DV, fn, *w)
        def pool(fn, *w): return Q.op(PO, fn, *w)

        def mm(o, l, r, start, stop, *w):
            return pe(lambda e: e.matmul(o, l, r, start=start, stop=stop), *w)

        def transpose(o, i, ident, *w):
            return pe(lambda e: e.transpose(o, i, ident), *w)

        def ts(o, i, s1, s2, o1, o2, *w, on=DV):
            return Q.op(on, lambda e: e.tensor_scalar(o, i, s1, s2, o1, o2) if o2 is not None
                        else e.tensor_scalar(o, i, s1, None, o1), *w)

        def tt(o, a, b, f, *w, on=DV):
            return Q.op(on, lambda e: e.tensor_tensor(o, a, b, f), *w)

        def stt(o, a, s, b, f, g, *w):
            return dve(lambda e: e.scalar_tensor_tensor(out=o, in0=a, scalar=s, in1=b, op0=f, op1=g), *w)

        def red(o, i, f, *w, absolute=False):
            return dve(lambda e: e.tensor_reduce(o, i, op=f, axis=AX.X, apply_absolute_value=absolute), *w)

        def fn(o, i, func, *w, **kw):
            return act(lambda e: e.activation(o, i, func, **kw), *w)

        def copy(on, o, i, *w):
            if on == AC:
                return fn(o, i, ACT.Copy, *w)
            return Q.op(on, lambda e: e.tensor_copy(o, i), *w)

        bfree = {b: [] for b in range(8)}

        z0 = pool(lambda e: e.memset(i32[:, :], 0.0))
        z1 = pool(lambda e: e.memset(ones[:, :], 1.0))
        k_i32 = pool(lambda e: e.affine_select(out=i32[:, :], in_=i32[:, :], compare_op=ALU.not_equal, fill=1.0,
                                               base=0, pattern=[[-1, 128]], channel_multiplier=1), z0)
        k_i16 = pool(lambda e: e.tensor_copy(i16[:, :], i32[:, :]), k_i32)
        k_one = z1
        k_fl = pool(lambda e: e.memset(fl[:, :], 0.0))
        k_st = pool(lambda e: e.memset(st[:, :], 0.0))
        bds = M2[:, 1536:2048].rearrange("p (k m) -> p k m", k=4)
        z_bd = pool(lambda e: e.memset(bds, 0.0))

        Wa, Wb = T3[:, 0:1024], T3[:, 1024:2048]
        NB = T3[:, 2048:3072].rearrange("p (t c) -> p t c", c=C)
        embt = [T3[64 * h:64 * h + D, 2048:3072] for h in range(2)]
        nbias = [M2[64 * h:64 * h + D, 1024:1024 + C] for h in range(2)]
        xr = x_in.rearrange("(t p) c -> t p c", p=128)
        atr = at_in.rearrange("(t p) i -> t p i", p=128)
        ar = a_in.rearrange("(t p) j -> t p j", p=128)

        x_ready, at_ready, b_done = [], [], []
        small = iter(s_small)

        def load_small(o, i, *w, on=SP):
            return Q.load(on, o, i, next(small), *w)

        l_bd = []

        def load_weights():
            nonlocal l_wa, l_wb, l_w2n, l_rows, l_b1, l_w1n
            l_wa = load_small(Wa, w0_in[0:128, :])
            l_wb = [load_small(T3[64 * h:64 * h + 64, 1024:2048], w0_in[128:192, :]) for h in range(2)]
            l_w2n = load_small(nrm[0:64, 2, :], w2_in)
            l_rows = load_small(rows[:, :, :], rows_in.rearrange("p (k c) -> p k c", c=C))
            l_b1 = load_small(b1c[:, :], b1_in)
            l_w1n = load_small(nrm[0:64, 0:2, :], w1_in.rearrange("p (k c) -> p k c", c=C))
            for k, src in enumerate((w1t_in[0:64, :], w1t_in[64:128, :], w2t_in, wl_in)):
                for h in range(2):
                    l_bd.append(load_small(bds[64 * h:64 * h + 64, k, 64 * h:64 * h + 64], src, z_bd))

        def load_embeddings():
            nonlocal l_emb, l_et
            l_et = [load_small(embt[h], embt_in[:, 1024 * h:1024 * h + 1024]) for h in range(2)]
            l_et += [load_small(nbias[h], w0b_in) for h in range(2)]
            l_emb = load_small(emb[:, :, :], emb_in.rearrange("(t p) d -> p t d", p=128))

        l_wa = l_wb = l_w2n = l_rows = l_b1 = l_w1n = l_emb = l_et = None

        def node_bias(h, b):
            for t in range(8):
                k_nb = mm(PS[:, b * 512 + t * C:b * 512 + t * C + C], embt[h][:, t * 128:(t + 1) * 128], nbias[h],
                          True, True, l_et, bfree[b])
            return k_nb

        SX = 64.0
        p0 = [None] * NT

        def xpart(S, jt):
            return S[:, jt, :].rearrange("p (b k c) -> p b k c", k=2, c=C)[:, :, 0, :]

        def tpart(S, jt):
            return S[:, jt, :].rearrange("p (b k c) -> p b k c", k=2, c=C)[:, :, 1, :]

        def split(jt, scale, *w):
            a = fn(xpart(S0, jt), grid(X[:, jt, :]), ACT.Copy, *w, scale=scale)
            return stt(xpart(S1, jt), grid(X[:, jt, :]), scale, xpart(S0, jt), ALU.mult, ALU.subtract, a, *w)

        ring_tok = [None] * 3
        nring = 0

        def ring(src):
            nonlocal nring
            k = nring % 3
            nring += 1
            return k, Q.load(SP, R[:, k, :], src, s_ring[k], ring_tok[k])

        last = {}

        def pair(b, it, jt, rh, rl, *w):
            mm(bank(b), Bm[:, jt, it * 128:(it + 1) * 128], rh(jt), jt == 0, False, *w)
            return mm(bank(b), Bm[:, jt, it * 128:(it + 1) * 128], rl(jt), False, jt == NT - 1)

        gload = {"n": 0, "tok": [None, None], "saved": None}

        def low_pass(tiles, banks, rh, *w):
            keep = Q.section
            Q.section = "G"
            for it, b in zip(tiles, banks):
                k = gload["n"] % 2
                gload["n"] += 1
                dst = R[:, 2, k * 1024:(k + 1) * 1024].bitcast(F16).rearrange("p (t i) -> p t i", i=128)
                ld = Q.load(SP, dst, blo[it], s_gb[k], gload["tok"][k], gload["saved"])
                for jt in range(NT):
                    m = mm(bank(b), dst[:, jt, :], rh(jt), False, False, ld, *w)
                gload["tok"][k] = m
            Q.section = keep

        class Tasks:

            def __init__(self, width):
                self.wait, self.active, self.turn, self.width = [], [], 0, width

            def add(self, gen, delay=0):
                self.wait.append((gen, self.turn + delay))

            def slot(self, force=False):
                self.turn += 1
                while len(self.active) < self.width and self.wait:
                    gen, due = self.wait.pop(0)
                    self.active.append([due, gen])
                if not self.active:
                    return False
                task = min(self.active, key=lambda x: x[0])
                if not force and self.turn < task[0]:
                    return True
                gap = next(task[1], None)
                if gap is None:
                    self.active.remove(task)
                else:
                    task[0] = self.turn + gap
                return True

            def until(self, cond):
                while not cond():
                    assert self.slot(True)

        def product(first, singles, banks, rh, rl, ready, evac, tasks, mid=None, every=4, w=(),
                    single_banks=None, order=None):
            fb = banks[:len(first)]
            n = 0
            for jt in range(NT):
                if jt == NT - 1:
                    tasks.until(lambda: ready(jt) is not None)
                    low_pass(first, fb, rh, [ready(j) for j in range(NT)], *w)
                for it, b in zip(first, fb):
                    if ready(jt) is None:
                        tasks.until(lambda: ready(jt) is not None)
                    t = pair(b, it, jt, rh, rl, ready(jt), bfree[b] if jt == 0 else None, *w)
                    last[it] = t
                    n += 2
                    if n % every == 0:
                        tasks.slot()
            if mid is not None:
                mid()
            for k in order or range(len(first)):
                evac(first[k], fb[k], last[first[k]])
            banks = single_banks or banks
            for k, it in enumerate(singles):
                b = banks[k % len(banks)]
                for jt in range(NT):
                    if jt == NT - 1:
                        low_pass([it], [b], rh, *w)
                    t = pair(b, it, jt, rh, rl, bfree[b] if jt == 0 else None, *w)
                    n += 2
                    if n % every == 0:
                        tasks.slot()
                evac(it, b, t)

        (cS, cX, cG, cS0, cWL, cW1, cW2, cLam, cSmax, cE, cEb, cV1, cSX, cVl,
         cB0, cT) = range(16)
        cs_sv, cs_sh, cs_ch, cs_cv = 16, 20, 23, 26
        cTmp = 32
        one_of = lambda k: sr[:, k:k + 1]

        def recip_scale(dst, src, num, *w):
            a = ts(col(dst), src, 1e-30, 1.0 / num, ALU.max, ALU.mult, *w)
            return dve(lambda e: e.reciprocal(col(dst), col(dst)), a)

        def weight_norms():
            d0 = tt(Wa[0:64, :], Wa[0:64, :], Wb[0:64, :], ALU.subtract, l_wa, l_wb)
            stc = lambda k, p=128: st[0:p, k:k + 1]
            w = [red(stc(0), Wa, ALU.max, d0, k_st, absolute=True),
                 red(stc(1), Wb, ALU.max, absolute=True),
                 red(stc(2), bds[:, 3, :], ALU.max, l_bd, absolute=True),
                 red(stc(3), bds[:, 0:2, :].rearrange("p k m -> p (k m)"), ALU.max, absolute=True),
                 red(stc(4), bds[:, 2, :], ALU.max, absolute=True),
                 red(stc(5, 64), nrm[0:64, 0, :], ALU.add, l_w1n, absolute=True),
                 red(stc(6, 64), nrm[0:64, 1, :], ALU.add, absolute=True),
                 red(stc(7, 64), nrm[0:64, 2, :], ALU.add, l_w2n, absolute=True),
                 red(stc(8), b1c[:, :], ALU.max, l_b1, absolute=True),
                 red(stc(9), rows[:, 1, :], ALU.max, l_rows, absolute=True),
                 red(stc(10), rows[:, 2, :], ALU.max, absolute=True)]
            return w

        def weight_halves():
            m0 = tt(col(cTmp), one_of(0), one_of(1), ALU.max, ar1)
            q0 = recip_scale(cS0, col(cTmp), 1024.0, m0)
            q1 = recip_scale(cWL, one_of(2), 1024.0, ar1)
            q2 = recip_scale(cW1, one_of(3), 1024.0, ar1)
            q3 = recip_scale(cW2, one_of(4), 1024.0, ar1)

            def halves(hi, lo, src, c, *w):
                a = fn(hi, src, ACT.Copy, *w, scale=c)
                return stt(lo, src, c, hi, ALU.mult, ALU.subtract, a, *w)

            h0 = halves(W01[:, 0, :], W01[:, 1, :], Wa, col(cS0), q0)
            h1 = halves(W2[:, 0, :], W2[:, 1, :], Wb, col(cS0), q0)
            h2 = halves(bdh[:, 0:2, :], bdl[:, 0:2, :], bds[:, 0:2, :], col(cW1), q2)
            h3 = halves(bdh[:, 2, :], bdl[:, 2, :], bds[:, 2, :], col(cW2), q3)
            h4 = halves(bdh[:, 3, :], bdl[:, 3, :], bds[:, 3, :], col(cWL), q1)
            w_ready = [h0, h1, h2, h3, h4]
            return q0, q1, q2, q3, w_ready

        junk = M2[:, 0:1024].bitcast(F16)
        jtok = None
        n_cnt = []

        for jt in range(NT):
            x_ready.append(Q.load(SP, X[:, jt, :], xr[jt], s_x[jt]))
            k, tok = ring(atr[jt])
            b01 = ts(Bm[:, jt, :], R[:, k, :], 0.0, None, ALU.not_equal, None, tok)
            ring_tok[k] = b01
            xt = split(jt, SX, x_ready[jt])
            mx = red(xm[:, jt:jt + 1], X[:, jt, :], ALU.max, absolute=True)
            p0[jt] = [b01, xt]
            jtok = fn(junk, Bm[:, jt, :], ACT.Copy, b01, jtok, accum_out=cnt[:, jt:jt + 1])
            n_cnt.append(jtok)
            if jt == 2:
                load_weights()
            if jt == 5:
                load_embeddings()
            if jt == 7:
                w = weight_norms()
                ar1 = pool(lambda e: e.partition_all_reduce(sr[:, :], st[:, :], 128, bass.bass_isa.ReduceOp.max), w)
            if jt == 11:
                q0, q1, q2, q3, w_ready = weight_halves()
                h0 = w_ready
                h1 = None

        def rx(S):
            return lambda jt: xpart(S, jt)

        st_r = [None] * NT
        st_a = [None] * NT

        def row_max(it):
            k, tok = ring(ar[it])
            a = red(rmax[:, it:it + 1], R[:, k, :], ALU.max, tok)
            n1 = ts(nr[:, it:it + 1], rmax[:, it:it + 1], -1.0, None, ALU.mult, None, a)
            ring_tok[k] = []
            st_a[it] = (k, tok, a, n1)

        def row_signs(it):
            nonlocal jtok
            k, tok, a, n1 = st_a[it]
            jtok = fn(junk, R[:, k, :], ACT.Sign, tok, n1, jtok, bias=nr[:, it:it + 1],
                      accum_out=sg1[:, it:it + 1])
            ring_tok[k] = [a, jtok]
            st_r[it] = [a, n1, jtok]

        t1_done = [None] * NT

        def evac1(it, b, tok):
            a = fn(tpart(S0, it), grid(bank(b)), ACT.Copy, tok, st_a[it][2] if Q.section is None else None,
                   scale=rmax[:, it:it + 1])
            t = stt(tpart(S1, it), grid(bank(b)), rmax[:, it:it + 1], tpart(S0, it), ALU.mult, ALU.subtract,
                    a, st_a[it][2] if Q.section is None else None)
            bfree[b] = [t]
            t1_done[it] = t

        c_nb = []

        def first_product():
            for jt in range(NT):
                for it in range(8):
                    last[it] = pair(it, it, jt, rx(S0), rx(S1), p0[jt], bfree[it] if jt == 0 else None)
            row_max(0)
            row_max(1)
            for it in range(8):
                evac1(it, it, last[it])
                row_signs(it)
                row_max(it + 2)
            for it in range(8, NT):
                b = it - 8
                for jt in range(NT):
                    t = pair(b, it, jt, rx(S0), rx(S1), bfree[b] if jt == 0 else None)
                evac1(it, b, t)
                if it == 10:
                    k_nb = [node_bias(h, 6 + h) for h in range(2)]
                if it == 12:
                    for h in range(2):
                        c_nb.append(copy(DV, T3[:, 2048 + 512 * h:2560 + 512 * h], bank(6 + h), k_nb))
                        bfree[6 + h] = [c_nb[h]]
                row_signs(it)
                if it + 2 < NT:
                    row_max(it + 2)
            return t

        pe_t1 = first_product()
        nb_all = []
        for it in range(NT):
            nb_all.append(tt(grid(X[:, it, :]), grid(X[:, it, :]), each_b(NB[:, it, :]), ALU.add,
                             c_nb, p0[it], mx, on=PO))

        def rt(S):
            return lambda jt: tpart(S, jt)

        def second_first():
            for jt in range(NT):
                if jt == NT - 1 and Q.section == "G":
                    low_pass([0, 1], [0, 1], rt(S0), t1_done)
                for it in (0, 1):
                    last[it] = pair(it, it, jt, rt(S0), rt(S1), t1_done[jt], bfree[it] if jt == 0 else None)
            return last[1]

        t2_first = second_first()

        allr = [t for x in st_r for t in x]
        a1 = stt(deg, sg1, float(N), rmax, ALU.add, ALU.mult, allr)
        a2 = stt(sg0, sg1, float(N), cnt, ALU.add, ALU.subtract, n_cnt, allr)
        a3 = red(col(49), sg0, ALU.add, a2)
        ar3 = pool(lambda e: e.partition_all_reduce(col(48), col(49), 128, bass.bass_isa.ReduceOp.add), a3)
        f = [red(fl[:, 1:2], nr, ALU.max, a1),
             red(fl[:, 2:3], rmax, ALU.max),
             red(fl[:, 3:4], deg, ALU.max),
             red(fl[:, 4:5], xm[:, :], ALU.max, mx)]
        ar2 = pool(lambda e: e.partition_all_reduce(fr[:, :], fl[:, :], 128, bass.bass_isa.ReduceOp.max), f, k_fl)
        c1 = copy(DV, col(cS), fr[:, 3:4], ar2)
        c2 = copy(DV, col(cX), fr[:, 4:5])
        c3 = dve(lambda e: e.memset(col(cSX), SX))

        def span(dst, *w):
            a = tt(col(dst), col(cS), col(cS), ALU.mult, *w)
            b = ts(col(dst), col(dst), 2.0, 1.0, ALU.mult, ALU.max, a)
            return tt(col(dst), col(dst), col(cX), ALU.mult, b)

        c4 = span(cTmp + 1, c1, c2)
        g = [ts(cs[:, 40:41], col(48), 0.0, None, ALU.not_equal, None, ar3),
             ts(cs[:, 41:42], fr[:, 1:2], 0.0, None, ALU.is_ge, None),
             ts(cs[:, 42:43], fr[:, 3:4], 8.0, None, ALU.is_gt, None),
             ts(cs[:, 43:44], col(cTmp + 1), 1000.0, None, ALU.is_gt, None, c4),
             ts(cs[:, 44:45], fr[:, 4:5], 1.0 / 64, None, ALU.is_lt, None)]
        g1 = red(fi[:, 0:1], cs[:, 40:45], ALU.max, g)
        g2 = ts(fi[:, 1:2], fr[:, 2:3], 0.5, None, ALU.is_gt, None)
        flags = {}

        def load_flags(eng):
            def do(e):
                v = e.value_load(fi[0:1, 0:1])
                u = e.value_load(fi[0:1, 1:2])
                flags[eng, "G"] = lambda: v
                flags[eng, "H"] = lambda: u
                return e.nop()
            return Q.op(eng, do, g1, g2)

        for eng in ENGINES:
            load_flags(eng)

        Q.section = "G"
        gt = [None] * 2
        gtd = None
        for it in range(NT):
            k = it % 2
            ld = Q.load(SP, R[:, k, :], ar[it], s_gr[k], gt[k], gtd, t2_first, g1)
            a = red(rmax[:, it:it + 1], R[:, k, :], ALU.max, ld, absolute=True)
            b = red(sg0[:, it:it + 1], R[:, k, :], ALU.add, absolute=True)
            c = red(deg[:, it:it + 1], R[:, k, :], ALU.add)
            gt[k] = c
        u = ts(rmax, rmax, 1e-30, 1.0 / 4096, ALU.max, ALU.mult, c)
        u = dve(lambda e: e.reciprocal(nr, rmax), u)
        u = red(fl[:, 3:4], sg0, ALU.max, u)
        u = pool(lambda e: e.partition_all_reduce(fr[:, :], fl[:, :], 128, bass.bass_isa.ReduceOp.max), u)
        u = copy(DV, col(cS), fr[:, 3:4], u)
        u = span(cTmp + 1, u)
        u = recip_scale(cSX, col(cTmp + 1), 8192.0, u)
        for jt in range(NT):
            ld = Q.load(SP, X[:, jt, :], xr[jt], s_gr[2], nb_all, u)
            u = split(jt, col(cSX), u, ld, t2_first)
            u = tt(grid(X[:, jt, :]), grid(X[:, jt, :]), each_b(NB[:, jt, :]), ALU.add, u)
        for it in range(NT):
            dg = M2[:, 0:128]
            u = ts(dg, i32[:, :], nr[:, it:it + 1], None, ALU.mult, None, u, k_i32, jtok)
            o = PS[:, (it % 16) * 128:(it % 16) * 128 + 128]
            u = mm(o, ones[:, :], dg, True, True, u, k_one, [bfree[x] for x in range(8)])
        u = copy(DV, R[:, 2, :], PS[:, 0:2048], u)
        qrow = R[:, 2, :]
        gx = u
        gw = [None, None]
        at_t = R[:, 1, :]
        lo_t = M2[:, 0:1024].bitcast(F16)
        for jt in range(NT):
            ld = Q.load(SP, R[:, 0, :], atr[jt], s_gr[2], u)
            a = tt(at_t, R[:, 0, :], qrow, ALU.mult, ld, u)
            b = copy(DV, Bm[:, jt, :], at_t, a)
            c = tt(lo_t, at_t, Bm[:, jt, :], ALU.subtract, b, gw[0])
            gw[0] = Q.load(SP, blo[:, :, jt, :].rearrange("t p i -> p t i"),
                           lo_t.rearrange("p (t i) -> p t i", i=128), s_gw, c)
            u = c
        gload["saved"] = [gw[0], u]

        ev = None
        for it in range(NT):
            b = it % 8
            for jt in range(NT):
                if jt == NT - 1:
                    low_pass([it], [b], rx(S0), u)
                t = pair(b, it, jt, rx(S0), rx(S1), u, gx, t1_done[it - 8] if it >= 8 else None)
            evac1(it, b, t)
        gdve = t1_done[NT - 1]
        u = second_first()
        pe(lambda e: e.nop(), u)
        dve(lambda e: e.nop(), gdve)
        act(lambda e: e.nop(), gdve)
        Q.section = None
        fence = dve(lambda e: e.nop())
        t2_first = [t2_first, pe(lambda e: e.nop())]
        for k in range(NT):
            t1_done[k] = fence
        for k in range(8):
            bfree[k] = [fence]

        e_r2 = ts(r2, rmax, 2.0, None, ALU.mult, None)
        u = tt(col(cE), col(cSX), col(cS0), ALU.mult, c1, c2, c3, q0)
        u = dve(lambda e: e.reciprocal(col(cE), col(cE)), u)
        e_emb = dve(lambda e: e.tensor_scalar(emb[:, :, :], emb[:, :, :], col(cE), None, ALU.mult), u, l_emb)

        ln_slots = [0, 1]
        sq_free = [None, None, None]

        def layernorm(it, y, cols, n=1, centred=False):
            slot = ln_slots.pop(0)
            w, m = 512 * n, 8 * n
            sq = (M2[:, (1024, 1536, 512)[slot]:] if n == 1 else T3[:, slot * 1024:])[:, 0:w]
            s = sm[:, slot, :]
            xt = X[:, it:it + n, :].rearrange("p t n -> p (t n)")

            def part(k):
                return s[:, k * m:(k + 1) * m]

            def wide(ap):
                return ap.unsqueeze(2).broadcast_to([128, m, C])

            xc = y
            if not centred:
                a = red(part(0), grid(xt), ALU.add, y, sq_free[slot])
                a = ts(part(1), part(0), -1.0 / C, None, ALU.mult, None, a)
                xc = tt(grid(xt), grid(xt), wide(part(1)), ALU.add, a)
            a = fn(sq, xt, ACT.Square, xc, sq_free[slot])
            yield None
            b = red(part(0), grid(sq), ALU.add, a, sq_free[slot])
            b = ts(part(2), part(0), cols[0], cols[1], ALU.mult, ALU.add, b, ln_ready)
            b = fn(part(3), part(2), ACT.Sqrt, b)
            yield None
            b = dve(lambda e: e.reciprocal(part(3), part(3)), b)
            c = tt(part(0), part(3), part(3), ALU.mult, b)
            c = tt(part(0), part(0), part(2), ALU.mult, c)
            c = ts(part(0), part(0), -0.5, 1.5, ALU.mult, ALU.add, c)
            b = tt(part(2), part(3), part(0), ALU.mult, c)
            t = tt(grid(xt), grid(xt), wide(part(2)), ALU.mult, b)
            sq_free[slot] = t
            ln_slots.append(slot)
            yield t

        TA = T3[:, :].bitcast(F16).rearrange("p (g k n) -> p g k n", k=8, n=128)
        ta_free = [[w_ready, fence], [nb_all[-1], w_ready, fence]]
        xsum = M2[:, 512:1024]
        erow = M2[:, 0:512]
        z = pool(lambda e: e.memset(xsum, 0.0), jtok, fence)
        xs_tok = [z]
        l0_done = [None] * NT
        tfree = [None, None]
        tbi = [0]
        ei = [0]
        done0 = [None] * NT
        t2_tok = [None] * NT
        ta_tok = [[] for _ in range(NT)]
        acc_tok = [None] * NT
        y1_free = [None, None]

        def t2_buf(it):
            return R[:, 0, :].bitcast(F16)[:, (it % 2) * 1024:(it % 2 + 1) * 1024]

        def evac2(it, b, tok):
            v = t2_buf(it).rearrange("p (b k c) -> p b k c", k=2, c=C)
            w = [tok, tfree[it % 2], e_r2, ring_tok]
            ps = grid(bank(b))
            for o in range(2):
                a = fn(v[:, o::2, o, :], ps[:, o::2, :], ACT.Copy, w, scale=r2[:, it:it + 1])
                w = []
            for o in range(2):
                t = stt(v[:, o::2, 1 - o, :], ps[:, o::2, :], r2[:, it:it + 1], v[:, o::2, o, :],
                        ALU.mult, ALU.subtract, a, e_r2)
            bfree[b] = [t]
            t2_tok[it] = t

        def transposes0(it, g):
            slot = it % 2
            src = (S0[:, it, :], S1[:, it, :], t2_buf(it))[g]
            b = 2 + tbi[0] % 2
            tbi[0] += 1
            for k in range(B):
                t = transpose(bank16(b)[:, k * 128:(k + 1) * 128], src[:, k * 128:(k + 1) * 128], i16[:, :],
                              bfree[b], t2_tok[it] if g == 2 else t1_done[it], k_i16)
            c = copy(AC, TA[:, 3 * slot + g, :, :].rearrange("p k n -> p (k n)"), bank16(b), t, ta_free[slot])
            bfree[b] = [c]
            ta_tok[it].append(c)
            if g == 2:
                tfree[slot] = t

        def round0(it, r):
            g, bp = divmod(r, 4)
            slot = it % 2
            TAs = TA[:, 3 * slot:3 * slot + 3]
            b0 = 4 + 2 * (ei[0] % 2)
            ei[0] += 1
            wc = slice(g * 512, (g + 1) * 512)
            for j in range(2):
                b, k = b0 + j, 2 * bp + j
                mm(bank(b), TAs[:, 0, k, :], W01[:, 0, wc], True, False, bfree[b], ta_tok[it], w_ready)
                mm(bank(b), TAs[:, 0, k, :], W01[:, 1, wc], False, False)
                mm(bank(b), TAs[:, 1, k, :], W01[:, 0, wc], False, False)
                mm(bank(b), TAs[:, 2, k, :], W2[:, 0, wc], False, False)
            for j in range(2):
                b, k = b0 + j, 2 * bp + j
                h = slice(64 * j, 64 * j + 64)
                t = mm(bank(b), TAs[h, 2, k, :], W2[h, 1, wc], False, True)
            ps = PS[:, b0 * 512:(b0 + 2) * 512].rearrange("p (b d o) -> p b d o", b=2, o=C)
            cols_ = slice(bp * 128, (bp + 1) * 128)
            xv = X[:, it, cols_].rearrange("p (b o) -> p b o", o=C)
            yv = R[:, 0, 1024 + 512 * slot:1536 + 512 * slot][:, cols_].rearrange("p (b o) -> p b o", o=C)
            y = [[acc_tok[it], nb_all[it]], [acc_tok[it], y1_free[slot]]]
            for d in range(8):
                k = d % 2
                e = emb[:, it, g * 8 + d:g * 8 + d + 1]
                if g == 0 and d == 1:
                    y[1] = ts(yv, ps[:, :, d, :], e, None, ALU.mult, None, t, y[1], e_emb)
                else:
                    v = (xv, yv)[k]
                    y[k] = stt(v, ps[:, :, d, :], e, v, ALU.mult, ALU.add, t, y[k], e_emb)
            bfree[b0] = list(y)
            bfree[b0 + 1] = list(y)
            acc_tok[it] = y[1]
            if r == 7:
                ta_free[slot] = t

        def finish0(it):
            slot = it % 2
            y = tt(X[:, it, :], X[:, it, :], R[:, 0, 1024 + 512 * slot:1536 + 512 * slot], ALU.add, acc_tok[it])
            y1_free[slot] = y
            for t in layernorm(it, y, LN_11):
                if t is None:
                    yield 3
            done0[it] = t
            if it < NT - 1:
                xs_tok[0] = tt(xsum, xsum, X[:, it, :], ALU.add, t, xs_tok[0], on=PO)

        evac2(0, 0, t2_first)
        evac2(1, 1, t2_first)
        for g in range(3):
            transposes0(0, g)
        fin = None
        for it in range(NT):
            for r in range(8):
                round0(it, r)
                if (it, r) == (0, 3):
                    u = ts(col(cTmp), col(cS), 1.0, 1.0 / 2048, ALU.add, ALU.mult)
                    lam = dve(lambda e: e.reciprocal(col(cLam), col(cTmp)), u)
                    u = tt(col(cEb), col(cLam), col(cLam), ALU.mult, lam)
                    e_epsL = ts(col(cEb), col(cEb), 1e-5, None, ALU.mult, None, u)
                    u = tt(col(cTmp), col(cLam), col(cLam), ALU.mult)
                    u = dve(lambda e: e.reciprocal(col(cTmp), col(cTmp)), u)
                    n_in1 = [ts(col(45), col(cTmp), 1.0 / C, None, ALU.mult, None, u),
                             ts(col(46), col(cTmp), 1e-5, None, ALU.mult, None),
                             ts(col(47), col(cTmp), 0.0, 1.0 / C, ALU.mult, ALU.add),
                             ts(col(48), col(cTmp), 0.0, 1e-5, ALU.mult, ALU.add)]
                    LN_11 = (col(47), col(48))
                    LN_1L = (col(45), col(46))
                    LN_LL = (col(45), col(48))
                    LN_L1 = (col(47), col(cEb))
                    ln_ready = n_in1 + [lam, e_epsL]
                if fin is not None and r in (1, 3, 5):
                    next(fin, None)
                if it + 1 < NT and r in (1, 3, 5):
                    transposes0(it + 1, r // 2)
                if it + 2 < NT:
                    b = it % 2
                    for jt in (2 * r, 2 * r + 1):
                        if jt == NT - 1:
                            low_pass([it + 2], [b], rt(S0))
                        t = pair(b, it + 2, jt, rt(S0), rt(S1), bfree[b] if jt == 0 else None)
                    if r == 7:
                        evac2(it + 2, b, t)
            if fin is not None:
                for _ in fin:
                    pass
            fin = finish0(it)
            if it == 0:
                u = ts(deg, deg, 1.0, None, ALU.add, None)
                u = ts(cw, deg, col(cWL), None, ALU.mult, None, u, q1)
                e_cw = dve(lambda e: e.reciprocal(cw, cw), u)
                e_lb = ts(b2s[:, 3, :], rows[:, 0, :], col(cLam), None, ALU.mult, None, lam)
                u = ts(col(cSmax), col(cS), 1.0, None, ALU.max, None)

                def v_scale(t, v, *w):
                    a = tt(col(50 + t), v, col(cSmax), ALU.mult, *w)
                    a = ts(col(50 + t), col(50 + t), 1e-30, 1.0 / 32768, ALU.max, ALU.mult, a)
                    return dve(lambda e: e.reciprocal(col(cs_sv + t), col(50 + t)), a)

                def step_scales(t, v, *w):
                    c = tt(col(35), one_of(6), col(cS), ALU.mult, *w)
                    c = tt(col(35), col(35), one_of(5), ALU.add, c)
                    c = tt(col(35), col(35), v, ALU.mult, c)
                    c = tt(col(35), col(35), one_of(8), ALU.add, c)
                    d = recip_scale(cs_sh + t, col(35), 32768.0, c)
                    f1 = tt(col(36), col(cs_sv + t), col(cW1), ALU.mult, d)
                    f1 = dve(lambda e: e.reciprocal(col(36), col(36)), f1)
                    f1 = tt(col(cs_ch + t), col(36), col(cs_sh + t), ALU.mult, f1)
                    f2 = tt(b1s[:, t:t + 1], b1c[:, :], col(cs_sh + t), ALU.mult)
                    g3 = tt(col(38), col(cs_sh + t), col(cW2), ALU.mult)
                    g3 = dve(lambda e: e.reciprocal(col(38), col(38)), g3)
                    if t < 2:
                        g4 = tt(col(37), one_of(7), col(35), ALU.mult)
                        g4 = tt(col(33), col(37), one_of(9), ALU.add, g4)
                        g4 = v_scale(t + 1, col(33), g4)
                        by = col(cs_sv + t + 1)
                    else:
                        by, g4 = col(cLam), None
                    k5 = tt(col(cs_cv + t), col(38), by, ALU.mult, g3, g4)
                    k6 = ts(b2s[:, t, :], rows[:, 1, :], by, None, ALU.mult, None, g4)
                    return [f1, f2, k5, k6]

                v0 = ts(col(32), one_of(10), 8.0, None, ALU.max, None, u)
                v0 = v_scale(0, col(32), v0)
                step_tok = {0: step_scales(0, col(32), v0)}
                scal = list(step_tok[0])
                u = dve(lambda e: e.reciprocal(col(39), col(cLam)))
                k_v0 = tt(col(cV1), col(cs_sv), col(39), ALU.mult, u)
                scal += [k_v0, e_lb, e_cw]
        for _ in fin:
            pass

        mm(bank(0), ones[:, :], xsum, True, False, xs_tok[0], bfree[0], k_one)
        mm_s = mm(bank(0), ones[:, :], X[:, NT - 1, :], False, True, done0[NT - 1])
        b = ts(M2[:, 1024:1536], bank(0), 1.0 / N, 0.0, ALU.mult, ALU.min, mm_s, jtok, sq_free)
        b = fn(M2[:, 1024:1536], M2[:, 1024:1536], ACT.Exp, b)
        a = ts(erow, bank(0), 1.0 / N, 0.0, ALU.mult, ALU.max, mm_s)
        bfree[0] = [a]
        k_er = stt(erow, M2[:, 1024:1536], -1.0, erow, ALU.add, ALU.add, a, b)
        def centre(ap, w):
            u = red(sm[:, 2, 0:8], grid(ap), ALU.add, w)
            u = ts(sm[:, 2, 8:16], sm[:, 2, 0:8], -1.0 / C, None, ALU.mult, None, u)
            return tt(grid(ap), grid(ap), spread(sm[:, 2, 8:16]), ALU.add, u)

        k_er = centre(erow, k_er)
        sq_free[:] = [k_er, k_er, k_er]
        ln_slots.append(2)
        l0_all = list(done0)

        Q.section = "H"
        sc = S0[:, :, :].rearrange("p t n -> p (t n)").bitcast(F32)
        hA, hrow, hU, hM = (sc[:, k * 2048:(k + 1) * 2048] for k in range(4))
        hP, hPT = R[:, 0, :], R[:, 1, :]
        E = S1[:, :, :].rearrange("p t n -> p (t n)").bitcast(F32).rearrange("p (t n) -> p t n", t=NT)
        s12 = W01[:, :, :].rearrange("p a n -> p (a n)").bitcast(F32)[:, 0:256].rearrange(
            "p (k t b) -> p k t b", k=2, b=B)
        u = [k_er, l0_all, h0]
        for it in range(NT):
            for k in range(2):
                u = tt(grid(hU[:, 0:512]), grid(X[:, it, :]), each_b(rows[:, 3 + k, :]), ALU.mult, u)
                u = red(s12[:, k, it, :], grid(hU[:, 0:512]), ALU.add, u)
        hb = bfree
        small8 = W01[:, 1, :].bitcast(F32)
        for b in range(B):
            for it in range(NT):
                u = ts(hP[:, 0:128], i32[:, :], s12[:, 1, it, b:b + 1], None, ALU.mult, None, u)
                u = mm(PS[:, it * 128:(it + 1) * 128], ones[:, :], hP[:, 0:128], True, True, u,
                       [bfree[x] for x in range(8)])
            u = copy(DV, hrow, PS[:, 0:2048], u)
            for it in range(NT):
                ld = Q.load(SP, hA, ar[it], s_h, u)
                a = ts(hU, hrow, s12[:, 0, it, b:b + 1], None, ALU.add, None, u)
                a = stt(hU, hU, 0.2, hU, ALU.mult, ALU.max, a)
                m = ts(hM, hA, 0.5, None, ALU.is_gt, None, ld, a)
                a = tt(hU, hU, hM, ALU.mult, m)
                m = ts(hM, hM, 1.0, 9000000000000000.0, ALU.subtract, ALU.mult, a)
                a = tt(hU, hU, hM, ALU.add, m)
                a = dve(lambda e: e.tensor_reduce(small8[:, 0:1], hU, op=ALU.max, axis=AX.X, negate=True), a)
                a = fn(hP, hU, ACT.Exp, a, bias=small8[:, 0:1], accum_out=small8[:, 1:2])
                for jt in range(NT):
                    t = transpose(PS[:, jt * 128:(jt + 1) * 128], hP[:, jt * 128:(jt + 1) * 128], i32[:, :], a)
                c = copy(DV, hPT, PS[:, 0:2048], t)
                for jt in range(NT):
                    t = mm(PS[:, 2048:2112], hPT[:, jt * 128:(jt + 1) * 128], X[:, jt, b * C:(b + 1) * C],
                           jt == 0, jt == NT - 1, c)
                d = dve(lambda e: e.reciprocal(small8[:, 2:3], small8[:, 1:2]), t)
                d = ts(small8[:, 64:128], PS[:, 2048:2112], small8[:, 2:3], 0.0, ALU.mult, ALU.min, d)
                f3 = fn(small8[:, 128:192], small8[:, 64:128], ACT.Exp, d)
                d = ts(small8[:, 64:128], PS[:, 2048:2112], small8[:, 2:3], 0.0, ALU.mult, ALU.max, f3)
                u = stt(E[:, it, b * C:(b + 1) * C], small8[:, 128:192], -1.0, small8[:, 64:128],
                        ALU.add, ALU.add, d)
        for it in range(NT):
            u = centre(X[:, it, :], tt(X[:, it, :], X[:, it, :], E[:, it, :], ALU.add, u))
        u = ts(erow, erow, 0.0, None, ALU.mult, None, u)
        dve(lambda e: e.nop(), u)
        Q.section = None
        fence = dve(lambda e: e.nop())
        fn(col(63), ones[:, 0:1], ACT.Sqrt)
        for k in range(8):
            bfree[k] = bfree[k] + [fence]

        sets = []
        for S in (S0, S1):
            v = S[:, :, :].rearrange("p t n -> p (t n)").rearrange("p (k t n) -> p k t n", k=2, n=BC)
            sets.append((v[:, 0], v[:, 1]))
        ready = [[None] * NT for _ in range(6)]
        tmp_free = {}

        tasks = Tasks(3)
        xready = [None] * NT

        units = [(0, 1), (1, 1)] + [(i, 2) for i in range(2, NT, 2)]

        def add_row(k):
            it, n = units[k]
            return tt(X[:, it:it + n, :], X[:, it:it + n, :], erow.unsqueeze(1).broadcast_to([128, n, BC]), ALU.add,
                      k_er, fence, on=PO if k else DV)

        y1_tok = [add_row(k) for k in range(4)]

        def work1(k):
            it, n = units[k]
            if k + 4 < len(units):
                y1_tok.append(add_row(k + 4))
            for t in layernorm(it, y1_tok[k], LN_1L, n=n, centred=True):
                if t is None:
                    yield 3
            H, L = sets[0]
            for i in range(it, it + n):
                a = copy(AC, H[:, i, :], X[:, i, :], t)
                b = tt(L[:, i, :], X[:, i, :], H[:, i, :], ALU.subtract, a, on=PO if i % 2 else DV)
                xready[i] = t
                ready[0][i] = [a, b]
            for i in range(6):
                ring_use[i] = t

        ring_use = {}
        gens = [work1(k) for k in range(len(units))]
        for k in (0, 0, 1, 0, 1, 2, 1):
            next(gens[k], None)
        for g in gens:
            tasks.add(g)

        def region(k):
            pieces = [T3[:, i * 512:(i + 1) * 512] for i in range(6)]
            w = [W01[:, i, :].bitcast(F32) for i in range(2)] + [W2[:, i, :].bitcast(F32) for i in range(2)]
            r = [R[:, 1, i * 512:(i + 1) * 512] for i in range(4)] + [R[:, 0, i * 512:(i + 1) * 512] for i in range(4)]
            return (pieces + w + r)[k]

        def halves_of(k):
            v = region(k).bitcast(F16)
            return v[:, 0:512], v[:, 512:1024]

        taux = [4, 5, 6, 7]
        nx = [0]

        def aux():
            b = taux[nx[0] % len(taux)]
            nx[0] += 1
            return b

        free = {}

        def transposed(dst, src, on, w):
            b = aux()
            for k in range(8):
                t = transpose(bank16(b)[:, k * 128:(k + 1) * 128], src[k], i16[:, :], bfree[b], w)
            c = copy(on, dst, bank16(b), t, free.get(id(dst)))
            bfree[b] = [c]
            return c, t

        def take(k):
            return ring_use.get(k)

        free_slots = [0, 1, 2]
        nz = [0]

        def evac_l2(it, b, tok):
            k0 = nz[0] % 2
            nz[0] += 1
            z = region(15 + k0)
            zh, zl = sets[1][0][:, it, :], sets[1][1][:, it, :]
            a = stt(z, bank(b), rmax[:, it:it + 1], X[:, it, :], ALU.mult, ALU.add, tok, xready[it],
                    take(15 + k0), fence)
            bfree[b] = [a]
            p = copy(AC, zh, z, a)
            q = tt(zl, z, zh, ALU.subtract, p, on=PO)
            xb = tt(grid(X[:, it, :]), grid(X[:, it, :]), each_b(b2s[:, 3, :]), ALU.add, a, e_lb, on=PO)
            ring_use[15 + k0] = [p, q]
            tasks.add(work2(it, zh, zl, p, q, xb), 3)

        def work2(it, zh, zl, p, q, xb):
            slot = free_slots.pop(0)
            k0 = 5 * slot
            zt = region(k0).bitcast(F16)
            ab = aux()
            for k in range(8):
                src = (zh, zl)[k // 4][:, (k % 4) * 128:(k % 4 + 1) * 128]
                t = transpose(bank16(ab)[:, k * 128:(k + 1) * 128], src, i16[:, :], bfree[ab], p, q)
            c = copy(AC, zt, bank16(ab), t, take(k0))
            bfree[ab] = [c]
            yield 4
            ab = aux()
            for k in range(4):
                o = bank(ab)[:, k * 128:(k + 1) * 128]
                lh, ll = zt[:, k * 128:(k + 1) * 128], zt[:, (k + 4) * 128:(k + 5) * 128]
                mm(o, lh, bdh[:, 3, :], True, False, bfree[ab], c, w_ready)
                mm(o, lh, bdl[:, 3, :], False, False)
                t = mm(o, ll, bdh[:, 3, :], False, True)
            ring_use[k0] = t
            free_slots.append(slot)
            y = stt(X[:, it, :], bank(ab), cw[:, it:it + 1], X[:, it, :], ALU.mult, ALU.add, t, xb, e_cw)
            bfree[ab] = [y]
            yield 3
            for t in layernorm(it, y, LN_LL):
                if t is None:
                    yield 3
            xready[it] = t
            H, L = sets[1]
            src = X[:, it, :]
            w = t
            if it == 0:
                src = region(17)
                w = copy(PO, src, X[:, 0, :], t)
                v = ts(grid(src[0:1, :]), rows[0:1, 2:3, :].broadcast_to([1, B, C]), col(cLam)[0:1, :], None,
                       ALU.mult, None, w)
                w = v
            p = fn(H[:, it, :], src, ACT.Copy, w, k_v0, scale=col(cV1))
            q = stt(L[:, it, :], src, col(cV1), H[:, it, :], ALU.mult, ALU.subtract, p)
            ready[1][it] = [p, q]

        def rs(S):
            return lambda jt: S[:, jt, :]

        product(list(range(7)), list(range(7, NT)), [0, 1, 2, 3, 4, 5, 6], rs(sets[0][0]), rs(sets[0][1]),
                lambda jt: ready[0][jt], evac_l2, tasks, every=4, single_banks=[0, 1, 2, 3], order=[0, 4, 1, 5, 2, 6, 3])

        outs = []
        orr = out.rearrange("b (t p) c -> t p b c", p=128)

        def make3(t):
            H0, L0 = sets[(t + 1) % 2]
            H1, L1 = sets[t % 2]

            def evac3(it, b, tok):
                eh, el = H1[:, it, :], L1[:, it, :]
                a = fn(eh, bank(b), ACT.Copy, tok, fence, scale=rmax[:, it:it + 1])
                q = stt(el, bank(b), rmax[:, it:it + 1], eh, ALU.mult, ALU.subtract, a)
                bfree[b] = [q]
                xb = None
                if t == 2:
                    xb = tt(grid(X[:, it, :]), grid(X[:, it, :]), each_b(b2s[:, 2, :]), ALU.add,
                            xready[it], step_tok[t], on=PO)
                tasks.add(work3(it, eh, el, q, xb), 3)

            def work3(it, eh, el, q, xb):
                slot = free_slots.pop(0)
                k0 = 5 * slot
                et = region(k0).bitcast(F16)
                vt = region(k0 + 1).bitcast(F16)
                hh = region(k0 + 2)
                h16, hl16 = halves_of(k0 + 3)
                vv = region(k0 + 4)
                ab = aux()
                for k in range(8):
                    src = (H0, L0)[k // 4][:, it, (k % 4) * 128:(k % 4 + 1) * 128]
                    tv = transpose(bank16(ab)[:, k * 128:(k + 1) * 128], src, i16[:, :], bfree[ab],
                                   ready[1 + t][it])
                cv = copy(AC, vt, bank16(ab), tv, take(k0 + 1))
                bfree[ab] = [cv]
                ab = aux()
                for k in range(8):
                    src = (eh, el)[k // 4][:, (k % 4) * 128:(k % 4 + 1) * 128]
                    te = transpose(bank16(ab)[:, k * 128:(k + 1) * 128], src, i16[:, :], bfree[ab], q)
                ce = copy(DV, et, bank16(ab), te, take(k0))
                bfree[ab] = [ce]
                yield 3
                ab = aux()
                for k in range(4):
                    o = bank(ab)[:, k * 128:(k + 1) * 128]
                    vh, vl = vt[:, k * 128:(k + 1) * 128], vt[:, (k + 4) * 128:(k + 5) * 128]
                    ehh, ell = et[:, k * 128:(k + 1) * 128], et[:, (k + 4) * 128:(k + 5) * 128]
                    mm(o, bdh[:, 0, :], vh, True, False, bfree[ab], ce, cv, w_ready)
                    mm(o, bdh[:, 0, :], vl, False, False)
                    mm(o, bdl[:, 0, :], vh, False, False)
                    mm(o, bdh[:, 1, :], ehh, False, False)
                    mm(o, bdh[:, 1, :], ell, False, False)
                    m = mm(o, bdl[:, 1, :], ehh, False, True)
                ring_use[k0] = m
                ring_use[k0 + 1] = m
                r = fn(hh, bank(ab), ACT.Relu, m, take(k0 + 2), step_tok[t],
                       scale=col(cs_ch + t), bias=b1s[:, t:t + 1])
                bfree[ab] = [r]
                p = copy(DV, h16, hh, r, take(k0 + 3))
                q = tt(hl16, hh, h16, ALU.subtract, p)
                ring_use[k0 + 2] = q
                yield 3
                ab = aux()
                for k in range(4):
                    o = bank(ab)[:, k * 128:(k + 1) * 128]
                    lh, ll = h16[:, k * 128:(k + 1) * 128], hl16[:, k * 128:(k + 1) * 128]
                    mm(o, lh, bdh[:, 2, :], True, False, bfree[ab], p, q)
                    mm(o, lh, bdl[:, 2, :], False, False)
                    m = mm(o, ll, bdh[:, 2, :], False, True)
                ring_use[k0 + 3] = m
                if t < 2:
                    v = stt(grid(vv), grid(bank(ab)), col(cs_cv + t), each_b(b2s[:, t, :]), ALU.mult, ALU.add,
                            m, take(k0 + 4), step_tok[t])
                    bfree[ab] = [v]
                    p = copy(AC, H1[:, it, :], vv, v)
                    vm[it] = red(vmx[:, it:it + 1], vv, ALU.max, v, absolute=True)
                    q = tt(L1[:, it, :], vv, H1[:, it, :], ALU.subtract, p)
                    ring_use[k0 + 4] = [q, vm[it]]
                    free_slots.append(slot)
                    ready[2 + t][it] = [p, q]
                else:
                    y = stt(X[:, it, :], bank(ab), col(cs_cv + t), X[:, it, :], ALU.mult, ALU.add, m, xb)
                    bfree[ab] = [y]
                    free_slots.append(slot)
                    yield 4
                    for tk in layernorm(it, y, LN_L1):
                        if tk is None:
                            yield 2
                    outs.append(Q.load(SP, orr[it], grid(X[:, it, :]), s_out[len(outs) % 2],
                                       tk, outs[-2] if len(outs) >= 2 else None))
            return evac3

        def measure(t):
            def mid():
                a = red(fl[:, 0:1], vmx[:, :], ALU.max, vm)
                b = pool(lambda e: e.partition_all_reduce(fr[:, 0:1], fl[:, 0:1], 128,
                                                          bass.bass_isa.ReduceOp.max), a)
                c = tt(col(32), fr[:, 0:1], col(50 + t), ALU.mult, b)
                step_tok[t] = step_scales(t, col(32), c)
            return mid

        for t in range(3):
            Hs, Ls = sets[(t + 1) % 2]
            product([0, 1, 2, 3], list(range(4, NT)), [0, 1, 2, 3], rs(Hs), rs(Ls),
                    lambda jt, t=t: ready[1 + t][jt], make3(t), tasks,
                    mid=measure(t) if t else None, every=4)
        while tasks.slot(True):
            pass
        Q.op(SP, lambda e: e.nop(), outs[-2:])

        Q.number()
        block = ctx.enter_context(nc.Block())

        @block.tensor
        def _(e):
            Q.replay(PE, e, flags)

        @block.vector
        def _(e):
            Q.replay(DV, e, flags)

        @block.scalar
        def _(e):
            Q.replay(AC, e, flags)

        @block.gpsimd
        def _(e):
            Q.replay(PO, e, flags)

        @block.sync
        def _(e):
            Q.replay(SP, e, flags)


_OUTS = [((8, 2048, 64), "float32")]


def kernel(**inputs):
    import concourse.bacc as _bacc
    from concourse.bass_utils import run_bass_kernel_spmd as _run

    def arr(name):
        return np.asarray(inputs[name])

    x, adj = arr("x"), arr("adj")
    emb, w0 = arr("L0_gnn_embedding"), arr("L0_gnn_weight")
    w1 = arr("L3_gnn_W1")
    rows = np.stack([arr("L2_gnn_b"), arr("L3_gnn_b2"), arr("L3_gnn_intervention_value")[0],
                     arr("L1_gnn_a")[:64, 0], arr("L1_gnn_a")[64:, 0]])
    b1 = arr("L3_gnn_b1")
    host = {
        "x_in": x.transpose(1, 0, 2).reshape(2048, 512),
        "at_in": adj.T,
        "a_in": adj,
        "embt_in": emb.T,
        "emb_in": emb,
        "w0_in": w0.transpose(1, 2, 0, 3).reshape(192, 1024),
        "w0b_in": arr("L0_gnn_bias"),
        "wl_in": arr("L2_gnn_W").T,
        "w1t_in": w1.T,
        "w2t_in": arr("L3_gnn_W2").T,
        "w1_in": w1,
        "w2_in": arr("L3_gnn_W2"),
        "b1_in": np.concatenate([b1, b1]).reshape(128, 1),
        "rows_in": np.tile(rows.reshape(1, 320), (128, 1)),
    }
    nc = _bacc.Bacc("TRN2", target_bir_lowering=False, num_devices=1, dynamic_dma_scratch_size=1024)
    arrays, args = {}, []
    for name, a in host.items():
        a = np.ascontiguousarray(a)
        arrays[name] = a
        args.append(nc.dram_tensor(name, a.shape, mybir.dt.from_np(a.dtype), kind="ExternalInput").ap())
    o = nc.dram_tensor("out_0", _OUTS[0][0], F32, kind="ExternalOutput").ap()
    gnn_kernel(nc, *args, o)
    r = _run(nc, [arrays], core_ids=[0])
    return r.results[0]["out_0"]
```
